# Optimizing a Trainium2 kernel written in Bass

```python
import numpy as np
import jax
import jax.numpy as jnp

def _softmax(x, axis=-1):
    return jax.nn.softmax(x, axis=axis)
def _gelu(x):
    return jax.nn.gelu(x, approximate=True)
def _silu(x):
    return jax.nn.silu(x)
def _sigmoid(x):
    return jax.nn.sigmoid(x)
def _layernorm(x, axis=-1, eps=1e-5):
    m = jnp.mean(x, axis=axis, keepdims=True)
    v = jnp.var(x, axis=axis, keepdims=True)
    return (x - m) / jnp.sqrt(v + eps)
def _scatter_add(tgt, idx, src, axis=0):
    return tgt.at[idx].add(src)
def _segment_sum(src, seg, n):
    return jax.ops.segment_sum(src, seg, n)

kernel_name = 'mk_conv_attn_hybrid_d2_conv_nchw128_4d3bc0'

def setup_inputs(seed: int = 0):
    np.random.seed(seed)
    _w = jnp.asarray
    def _rec_inputs():
        import jax
        import jax.numpy as jnp
        _gk = jax.random.key(seed)
        x = -0.0005207 + 1.001 * jax.random.normal(jax.random.fold_in(_gk, 1), (16, 128, 32, 32), jnp.float32)
        return x
    x = _rec_inputs()
    def _L0_conv_setup():
        import jax, jax.numpy as jnp
        import numpy as np
        EPS = 1e-05

        def adder2d(x, w, stride=1, padding=1):
            cout, _, kh, kw = w.shape
            patches = jax.lax.conv_general_dilated_patches(x, (kh, kw), (stride, stride), ((padding, padding), (padding, padding)))
            wf = w.reshape(cout, -1)

            @jax.checkpoint
            def per_out(wc):
                return -jnp.sum(jnp.abs(patches - wc[None, :, None, None]), axis=1)
            out = jax.lax.map(per_out, wf)
            return jnp.transpose(out, (1, 0, 2, 3))

        def bn_inference(x, gamma, beta, mean, var):
            inv = gamma * jax.lax.rsqrt(var + EPS)
            return x * inv[None, :, None, None] + (beta - mean * inv)[None, :, None, None]
        key = jax.random.key(seed)
        ks = jax.random.split(key, 16)
        N, C, H, W = (16, 128, 32, 32)
        R = C // 16
        return {'x': jax.random.normal(ks[0], (N, C, H, W), jnp.float32), 'w1': jax.random.normal(ks[1], (C, C, 3, 3), jnp.float32) * 0.05, 'bn1_gamma': jax.random.uniform(ks[2], (C,), jnp.float32), 'bn1_beta': jax.random.normal(ks[3], (C,), jnp.float32) * 0.1, 'bn1_mean': jax.random.normal(ks[4], (C,), jnp.float32) * 0.1, 'bn1_var': jax.random.uniform(ks[5], (C,), jnp.float32), 'w2': jax.random.normal(ks[6], (C, C, 3, 3), jnp.float32) * 0.05, 'bn2_gamma': jax.random.uniform(ks[7], (C,), jnp.float32), 'bn2_beta': jax.random.normal(ks[8], (C,), jnp.float32) * 0.1, 'bn2_mean': jax.random.normal(ks[9], (C,), jnp.float32) * 0.1, 'bn2_var': jax.random.uniform(ks[10], (C,), jnp.float32), 'fc1_w': jax.random.normal(ks[11], (R, C), jnp.float32) * 0.1, 'fc1_b': jax.random.normal(ks[12], (R,), jnp.float32) * 0.1, 'fc2_w': jax.random.normal(ks[13], (C, R), jnp.float32) * 0.1, 'fc2_b': jax.random.normal(ks[14], (C,), jnp.float32) * 0.1}
    _L0_conv_all = _L0_conv_setup()
    _L0_conv_in = {k: v for k, v in _L0_conv_all.items() if k in ('w1', 'bn1_gamma', 'bn1_beta', 'bn1_mean', 'bn1_var', 'w2', 'bn2_gamma', 'bn2_beta', 'bn2_mean', 'bn2_var', 'fc1_w', 'fc1_b', 'fc2_w', 'fc2_b', )}
    del _L0_conv_all

    def _L1_attn_setup():
        import jax, jax.numpy as jnp
        import numpy as np
        B, L, D = (4, 512, 128)
        ATTN_WIDTH = 3
        EPS = 1e-08
        key = jax.random.key(seed)
        ks = jax.random.split(key, 4)
        lim = float(np.sqrt(6.0 / (D + D)))
        lim_a = float(np.sqrt(6.0 / (D + 1)))
        return {'inputs': jax.random.normal(ks[0], (B, L, D), dtype=jnp.float32), 'Wt': jax.random.uniform(ks[1], (D, D), jnp.float32, -lim, lim), 'Wx': jax.random.uniform(ks[2], (D, D), jnp.float32, -lim, lim), 'Wa': jax.random.uniform(ks[3], (D, 1), jnp.float32, -lim_a, lim_a), 'bh': jnp.zeros((D,), jnp.float32), 'ba': jnp.zeros((1,), jnp.float32)}
    _L1_attn_all = _L1_attn_setup()
    _L1_attn_in = {k: v for k, v in _L1_attn_all.items() if k in ('Wt', 'Wx', 'Wa', 'bh', 'ba', )}
    del _L1_attn_all

    def _L1_ffn_setup():
        import jax, jax.numpy as jnp
        import numpy as np
        PADDED_SL = 8192
        TEMPERATURE = 1.0
        SIGMA_POW = 0.25

        def _stu_conv(phi, u, n):
            b, sl, d = u.shape
            sgn = jnp.where(jnp.arange(sl) % 2 == 0, 1.0, -1.0).astype(u.dtype)
            sgn3 = sgn[None, :, None]
            Vf = jnp.fft.rfft(phi, n=n, axis=0)
            Uf_p = jnp.fft.rfft(u, n=n, axis=1)
            Uf_m = jnp.fft.rfft(u * sgn3, n=n, axis=1)
            U_plus = jnp.fft.irfft(Vf[None, :, :, None] * Uf_p[:, :, None, :], n=n, axis=1)[:, :sl]
            U_minus = jnp.fft.irfft(Vf[None, :, :, None] * Uf_m[:, :, None, :], n=n, axis=1)[:, :sl]
            U_minus = U_minus * sgn[None, :, None, None]
            return (U_plus, U_minus)

        def _compute_spectral(u, sigma, phi, Mpp, Mpm):
            U_plus, U_minus = _stu_conv(phi, u, PADDED_SL)
            s = sigma ** SIGMA_POW
            out = jnp.einsum('btkd,k,kde->bte', U_plus, s, Mpp)
            out = out + jnp.einsum('btkd,k,kde->bte', U_minus, s, Mpm)
            return out

        def _compute_ar_u(Mu, u):
            sl = u.shape[1]
            out = jnp.zeros(u.shape[:2] + (Mu.shape[-1],), dtype=u.dtype)
            for i in range(Mu.shape[0]):
                ui = jnp.pad(u, ((0, 0), (i, 0), (0, 0)))[:, :sl]
                out = out + jnp.einsum('btd,de->bte', ui, Mu[i])
            return out

        def _stu(u, sigma, phi, Mu, Mpp, Mpm):
            return _compute_spectral(u, sigma, phi, Mpp, Mpm) + _compute_ar_u(Mu, u)
        key = jax.random.key(seed)
        ks = jax.random.split(key, 8)
        b, sl, d, K, k_u = (2, 4096, 128, 16, 3)
        x = jax.random.normal(ks[0], (b, sl, d), dtype=jnp.float32)
        sigma = jax.random.uniform(ks[1], (K,), dtype=jnp.float32, minval=0.001, maxval=1.0)
        phi = jax.random.normal(ks[2], (sl, K), dtype=jnp.float32) / np.sqrt(sl)
        M_u = jax.random.normal(ks[3], (4, k_u, d, d), dtype=jnp.float32) * 0.02
        M_phi_plus = jax.random.normal(ks[4], (4, K, d, d), dtype=jnp.float32) * 0.02
        M_phi_minus = jax.random.normal(ks[5], (4, K, d, d), dtype=jnp.float32) * 0.02
        log_weights = jnp.ones((4,), dtype=jnp.float32)
        u01 = jax.random.uniform(ks[6], (4,), dtype=jnp.float32, minval=1e-06, maxval=1.0 - 1e-06)
        gumbel = -jnp.log(-jnp.log(u01))
        return {'x': x, 'sigma': sigma, 'phi': phi, 'M_u': M_u, 'M_phi_plus': M_phi_plus, 'M_phi_minus': M_phi_minus, 'log_weights': log_weights, 'gumbel': gumbel}
    _L1_ffn_all = _L1_ffn_setup()
    _L1_ffn_in = {k: v for k, v in _L1_ffn_all.items() if k in ('sigma', 'phi', 'M_u', 'M_phi_plus', 'M_phi_minus', 'log_weights', 'gumbel', )}
    del _L1_ffn_all

    return {
        "x": x,
        "L0_conv_w1": _L0_conv_in["w1"],
        "L0_conv_bn1_gamma": _L0_conv_in["bn1_gamma"],
        "L0_conv_bn1_beta": _L0_conv_in["bn1_beta"],
        "L0_conv_bn1_mean": _L0_conv_in["bn1_mean"],
        "L0_conv_bn1_var": _L0_conv_in["bn1_var"],
        "L0_conv_w2": _L0_conv_in["w2"],
        "L0_conv_bn2_gamma": _L0_conv_in["bn2_gamma"],
        "L0_conv_bn2_beta": _L0_conv_in["bn2_beta"],
        "L0_conv_bn2_mean": _L0_conv_in["bn2_mean"],
        "L0_conv_bn2_var": _L0_conv_in["bn2_var"],
        "L0_conv_fc1_w": _L0_conv_in["fc1_w"],
        "L0_conv_fc1_b": _L0_conv_in["fc1_b"],
        "L0_conv_fc2_w": _L0_conv_in["fc2_w"],
        "L0_conv_fc2_b": _L0_conv_in["fc2_b"],
        "L1_attn_Wt": _L1_attn_in["Wt"],
        "L1_attn_Wx": _L1_attn_in["Wx"],
        "L1_attn_Wa": _L1_attn_in["Wa"],
        "L1_attn_bh": _L1_attn_in["bh"],
        "L1_attn_ba": _L1_attn_in["ba"],
        "L1_ffn_sigma": _L1_ffn_in["sigma"],
        "L1_ffn_phi": _L1_ffn_in["phi"],
        "L1_ffn_M_u": _L1_ffn_in["M_u"],
        "L1_ffn_M_phi_plus": _L1_ffn_in["M_phi_plus"],
        "L1_ffn_M_phi_minus": _L1_ffn_in["M_phi_minus"],
        "L1_ffn_log_weights": _L1_ffn_in["log_weights"],
        "L1_ffn_gumbel": _L1_ffn_in["gumbel"],
    }

def reference(x, L0_conv_w1, L0_conv_bn1_gamma, L0_conv_bn1_beta, L0_conv_bn1_mean, L0_conv_bn1_var, L0_conv_w2, L0_conv_bn2_gamma, L0_conv_bn2_beta, L0_conv_bn2_mean, L0_conv_bn2_var, L0_conv_fc1_w, L0_conv_fc1_b, L0_conv_fc2_w, L0_conv_fc2_b, L1_attn_Wt, L1_attn_Wx, L1_attn_Wa, L1_attn_bh, L1_attn_ba, L1_ffn_sigma, L1_ffn_phi, L1_ffn_M_u, L1_ffn_M_phi_plus, L1_ffn_M_phi_minus, L1_ffn_log_weights, L1_ffn_gumbel):
    import jax
    import jax.numpy as jnp
    def _L0_conv_ref(x, w1, bn1_gamma, bn1_beta, bn1_mean, bn1_var, w2, bn2_gamma, bn2_beta, bn2_mean, bn2_var, fc1_w, fc1_b, fc2_w, fc2_b):
        import jax, jax.numpy as jnp
        import numpy as np
        EPS = 1e-05

        def adder2d(x, w, stride=1, padding=1):
            cout, _, kh, kw = w.shape
            patches = jax.lax.conv_general_dilated_patches(x, (kh, kw), (stride, stride), ((padding, padding), (padding, padding)))
            wf = w.reshape(cout, -1)

            @jax.checkpoint
            def per_out(wc):
                return -jnp.sum(jnp.abs(patches - wc[None, :, None, None]), axis=1)
            out = jax.lax.map(per_out, wf)
            return jnp.transpose(out, (1, 0, 2, 3))

        def bn_inference(x, gamma, beta, mean, var):
            inv = gamma * jax.lax.rsqrt(var + EPS)
            return x * inv[None, :, None, None] + (beta - mean * inv)[None, :, None, None]
        out = jax.nn.relu(bn_inference(adder2d(x, w1), bn1_gamma, bn1_beta, bn1_mean, bn1_var))
        out = bn_inference(adder2d(out, w2), bn2_gamma, bn2_beta, bn2_mean, bn2_var)
        s = jnp.mean(out, axis=(2, 3))
        s = jax.nn.relu(s @ fc1_w.T + fc1_b)
        s = jax.nn.sigmoid(s @ fc2_w.T + fc2_b)
        out = out * s[:, :, None, None]
        return jax.nn.relu(out + x)

    def _L1_attn_ref(inputs, Wt, Wx, Wa, bh, ba):
        import jax, jax.numpy as jnp
        import numpy as np
        B, L, D = (4, 512, 128)
        ATTN_WIDTH = 3
        EPS = 1e-08
        b, n, d = inputs.shape
        q = inputs @ Wt
        k = inputs @ Wx
        h = jnp.tanh(q[:, :, None, :] + k[:, None, :, :] + bh)
        e = jnp.einsum('bqkd,d->bqk', h, Wa[:, 0]) + ba[0]
        e = jnp.exp(e - jnp.max(e, axis=-1, keepdims=True))
        idx = jnp.arange(n)
        lower = idx - ATTN_WIDTH // 2
        mask = (idx[None, :] >= lower[:, None]) & (idx[None, :] < lower[:, None] + ATTN_WIDTH)
        e = e * mask[None].astype(e.dtype)
        s = jnp.sum(e, axis=-1, keepdims=True)
        a = e / (s + EPS)
        return jnp.einsum('bqk,bkd->bqd', a, inputs)

    def _L1_ffn_ref(x, sigma, phi, M_u, M_phi_plus, M_phi_minus, log_weights, gumbel):
        import jax, jax.numpy as jnp
        import numpy as np
        PADDED_SL = 8192
        TEMPERATURE = 1.0
        SIGMA_POW = 0.25

        def _stu_conv(phi, u, n):
            b, sl, d = u.shape
            sgn = jnp.where(jnp.arange(sl) % 2 == 0, 1.0, -1.0).astype(u.dtype)
            sgn3 = sgn[None, :, None]
            Vf = jnp.fft.rfft(phi, n=n, axis=0)
            Uf_p = jnp.fft.rfft(u, n=n, axis=1)
            Uf_m = jnp.fft.rfft(u * sgn3, n=n, axis=1)
            U_plus = jnp.fft.irfft(Vf[None, :, :, None] * Uf_p[:, :, None, :], n=n, axis=1)[:, :sl]
            U_minus = jnp.fft.irfft(Vf[None, :, :, None] * Uf_m[:, :, None, :], n=n, axis=1)[:, :sl]
            U_minus = U_minus * sgn[None, :, None, None]
            return (U_plus, U_minus)

        def _compute_spectral(u, sigma, phi, Mpp, Mpm):
            U_plus, U_minus = _stu_conv(phi, u, PADDED_SL)
            s = sigma ** SIGMA_POW
            out = jnp.einsum('btkd,k,kde->bte', U_plus, s, Mpp)
            out = out + jnp.einsum('btkd,k,kde->bte', U_minus, s, Mpm)
            return out

        def _compute_ar_u(Mu, u):
            sl = u.shape[1]
            out = jnp.zeros(u.shape[:2] + (Mu.shape[-1],), dtype=u.dtype)
            for i in range(Mu.shape[0]):
                ui = jnp.pad(u, ((0, 0), (i, 0), (0, 0)))[:, :sl]
                out = out + jnp.einsum('btd,de->bte', ui, Mu[i])
            return out

        def _stu(u, sigma, phi, Mu, Mpp, Mpm):
            return _compute_spectral(u, sigma, phi, Mpp, Mpm) + _compute_ar_u(Mu, u)
        T = x.shape[1]
        outs = []
        for i, frac in enumerate((1, 2, 4, 8)):
            xi = x[:, :T // frac]
            si = _stu(xi, sigma, phi, M_u[i], M_phi_plus[i], M_phi_minus[i])
            si = jnp.pad(si, ((0, 0), (0, T - si.shape[1]), (0, 0)))
            outs.append(si)
        y_soft = jax.nn.softmax((log_weights + gumbel) / TEMPERATURE)
        y_hard = jax.nn.one_hot(jnp.argmax(y_soft), 4, dtype=y_soft.dtype)
        weights = y_hard - jax.lax.stop_gradient(y_soft) + y_soft
        stacked = jnp.stack(outs, axis=-1)
        return jnp.sum(stacked * weights, axis=-1)

    def _gn(v, G=32, eps=1e-5):
        B_, C_, H_, W_ = v.shape
        g = v.reshape(B_, G, C_ // G, H_, W_)
        m = jnp.mean(g, axis=(2, 3, 4), keepdims=True)
        s = jnp.var(g, axis=(2, 3, 4), keepdims=True)
        return ((g - m) / jnp.sqrt(s + eps)).reshape(v.shape)

    def _ln_c(v, eps=1e-6):
        m = jnp.mean(v, axis=1, keepdims=True)
        s = jnp.var(v, axis=1, keepdims=True)
        return (v - m) / jnp.sqrt(s + eps)

    def _ln_t(v, eps=1e-5):
        m = jnp.mean(v, axis=-1, keepdims=True)
        s = jnp.var(v, axis=-1, keepdims=True)
        return (v - m) / jnp.sqrt(s + eps)

    def _to_tokens(v):
        B_, C_, H_, W_ = v.shape
        return v.reshape(B_, C_, H_ * W_).transpose(0, 2, 1)
    def _from_tokens(t, like):
        B_, C_, H_, W_ = like.shape
        return t.transpose(0, 2, 1).reshape(B_, C_, H_, W_)

    x = _L0_conv_ref(x, L0_conv_w1, L0_conv_bn1_gamma, L0_conv_bn1_beta, L0_conv_bn1_mean, L0_conv_bn1_var, L0_conv_w2, L0_conv_bn2_gamma, L0_conv_bn2_beta, L0_conv_bn2_mean, L0_conv_bn2_var, L0_conv_fc1_w, L0_conv_fc1_b, L0_conv_fc2_w, L0_conv_fc2_b)
    t = _to_tokens(x)
    t = t + _L1_attn_ref(_ln_t(t), L1_attn_Wt, L1_attn_Wx, L1_attn_Wa, L1_attn_bh, L1_attn_ba)
    t = t + _L1_ffn_ref(_ln_t(t), L1_ffn_sigma, L1_ffn_phi, L1_ffn_M_u, L1_ffn_M_phi_plus, L1_ffn_M_phi_minus, L1_ffn_log_weights, L1_ffn_gumbel)
    x = _from_tokens(t, x)
    return x


_drawn_inputs = setup_inputs


def setup_inputs(seed=0):
    import zlib

    import numpy as np

    out = dict(_drawn_inputs(seed))
    spreads = {'L1_attn_bh': (0.0, 0.504), 'L1_ffn_log_weights': (1.0, 0.2)}
    factors = {'L0_conv_bn2_beta': 4.086, 'L0_conv_bn2_mean': 5.295, 'L0_conv_fc1_b': 41.776}
    for name, (base, spread) in spreads.items():
        noise = np.random.default_rng([zlib.crc32(name.encode()), seed]).standard_normal(out[name].shape)
        drawn = base * np.exp(spread * noise) if base else spread * noise
        out[name] = jnp.asarray(drawn.astype(out[name].dtype))
    for name, factor in factors.items():
        out[name] = (out[name] * factor).astype(out[name].dtype)
    return out
```

```python
import concourse.bass as bass
from concourse import mybir
from contextlib import ExitStack

FP32 = mybir.dt.float32
BF16 = mybir.dt.bfloat16
ALU = mybir.AluOpType
ACT = mybir.ActivationFunctionType
AX = mybir.AxisListType

P = 128
H = W = 32
HW = H * W
PW = W + 2
PAIR = 2
PAIRPOS = PAIR * HW
TAPS = 9
GROUPS = 4
ROWS = P // GROUPS
PARTS = 4
TILES = ROWS // PARTS
SLOTS = TAPS * GROUPS
RING = 9
RING_CREDIT = 3
ITER_QUADS = TAPS
CONV_QUADS = TILES * PARTS * ITER_QUADS
TQUADS = 8
TILE_TQUADS = PARTS * TQUADS
TRING = 8
BANK = 512
BN_EPS = 1e-5
LN_EPS = 1e-5
ATTN_EPS = 1e-8
OUTSIDE = -1e30
EP = HW + 2
NF = 16
HALF = HW // 2
TB = HALF // P
FW = HALF + 1
NK = 2 * NF
NLEN = 4
SEGS = [(HALF // 2, HALF), (HALF // 4, HALF // 2), (HALF // 8, HALF // 4), (0, HALF // 8)]
ACT_SHARE = {False: 14, True: 4}


def act_slots(n):
    return {int((j + 0.5) * SLOTS / n) for j in range(n)}


class Steps:

    def __init__(self, sem, per, before, offset=0):
        self.sem, self.per, self.base, self.n = sem, per, before * per + offset, 0

    def did(self, instruction):
        instruction.then_inc(self.sem, 1)
        self.n += 1
        assert self.n <= self.per

    def at(self, n):
        return self.base + n

    def link(self, engine, instruction):
        self.did(instruction)
        engine.wait_ge(self.sem, self.base + self.n)


def build(nc, a, out):
    n_img = a["x"].shape[0]
    pairs = n_img // PAIR
    x_dram = a["x"].rearrange("(g n) c h w -> g c n (h w)", n=PAIR)
    out_dram = out.rearrange("n c h w -> n c (h w)")
    mid_dram = nc.dram_tensor("tokens_after_attention", [n_img, P, HW], FP32, kind="Internal").ap()
    FROW = P + HALF
    filt = nc.dram_tensor("padded_filters", [NK, FROW], FP32, kind="Internal")
    filt_dram = filt.ap()

    with ExitStack() as ctx:
        def sem(name):
            return ctx.enter_context(nc.semaphore(name))

        arena = ctx.enter_context(nc.sbuf_tensor("arena", [P, 53100], FP32))
        place = {"at": 0, "top": 0}

        def take(*shape):
            size = 1
            for s in shape:
                size *= s
            o = place["at"]
            place["at"] += size
            assert place["at"] <= 53100, place
            v = arena[:, o:o + size]
            if len(shape) == 1:
                return v
            names = "abcd"[:len(shape)]
            return v.rearrange("p (%s) -> p %s" % (" ".join(names), " ".join(names)),
                               **{n: s for n, s in zip(names[1:], shape[1:])})

        ident = take(P)
        sums = take(P)
        means = take(P)
        nhalf = take(P)
        zeros = take(BANK)
        wlen = take(NLEN)
        mu = take(3, NLEN, P)
        small = take(64)
        kept = place["at"]
        ring = take(RING, PAIRPOS)
        tring = take(TRING, HW)
        xp = take(PAIR, PW, PW)
        x2p = take(PAIR, PW, PW)
        xn = take(PAIRPOS)
        box_rows = take(PAIR, PW, W)
        box = take(PAIR, H, W)
        nw = take(2, TAPS, P)
        kT = take(PAIR, HW)
        qT = take(PAIR, HW)
        xl = take(PAIR, EP)
        tt = take(PAIR, HW)
        ep = take(EP)
        prod = take(3, P)
        ones_hot = take(2 * ROWS - 1)
        wa_hot = take(2 * ROWS - 1)
        ones_now = take(ROWS + PARTS - 1)
        wt_sb, wx_sb = take(P), take(P)
        fc1T, fc2T = take(8), take(P)
        colv = take(24)
        scores3 = take(TILES, 3)
        expd = take(TILES, 3)
        probs = take(TILES, 3)
        used1 = place["at"]
        place["at"] = kept
        toep = take(NK, FW)
        mf = take(NF, 2, NLEN, P)
        raw = take(2, 2, NLEN, P)
        xm = take(2, NLEN, P)
        tok = take(HW)
        uT = take(2, FW)
        uR = take(2, HALF)
        u = take(2, TB, P)
        conv_out = take(3, 2, HALF)
        ln_a, ln_b = take(HW), take(HW)
        result = take(HW)
        used2 = place["at"]
        w_raw = [ring[:, c, 0:TAPS * P] for c in (0, 1)]
        phiT = ring[0:NK, 2, 0:FROW]
        mu_raw = ring[:, 3, 0:NLEN * 3 * P].rearrange("p (i t e) -> p i t e", i=NLEN, t=3)
        sig = small[0:NK, 0:1]
        row = small[0:1, 8:40].rearrange("p (a b) -> p a b", b=4)
        m_cur, e_cur = small[:, 40:41], small[:, 41:44]
        s8, r8 = small[:, 44:52], small[:, 52:60]
        col = {n: colv[:, i:i + 1] for i, n in enumerate(
            ["g1", "b1", "m1", "v1", "g2", "b2", "m2", "v2", "fc2b", "bh", "wa", "ba", "sc1", "bi1",
             "sc2", "bi2", "sw", "fc1b", "tmp", "sg0", "sg1", "th0", "th1", "bh_"])}
        pooled, z1, gate, th = small[:, 60:62], small[0:8, 62:64], colv[:, 19:21], colv[:, 21:23]

        acc = ctx.enter_context(nc.psum_tensor("acc", [P, PAIRPOS], FP32))
        e_ps = ctx.enter_context(nc.psum_tensor("e_ps", [P, HW], FP32))
        misc = ctx.enter_context(nc.psum_tensor("misc", [P, HW], FP32))

        loaded = sem("loaded")
        consts = sem("consts")
        pe_setup, dve_setup, act_setup = sem("pe_setup"), sem("dve_setup"), sem("act_setup")
        filters_stored = sem("filters_stored")
        x_loaded, x_padded, queries_ready = sem("x_loaded"), sem("x_padded"), sem("queries_ready")
        filters_loaded = sem("filters_loaded")
        relu_dve, relu_act, relus_used = sem("relu_dve"), sem("relu_act"), sem("relu_quads_used")
        hot_ready = sem("hot_ready")
        tanh_ready, tanhs_used = sem("tanh_ready"), sem("tanh_quads_used")
        score_step = sem("score_step")
        box_step = sem("box_step")
        sums_closed = sem("sums_closed")
        x2_ready = sem("x2_ready")
        fin_pe, fin_dve, fin_act = sem("finish_pe"), sem("finish_dve"), sem("finish_act")
        post_pe, post_dve, post_act = sem("post_pe"), sem("post_dve"), sem("post_act")
        mid_stored = sem("mid_stored")
        toep_loaded = sem("toeplitz_loaded")
        m_loaded, m_step = [sem("m_loaded0"), sem("m_loaded1")], sem("m_step")
        tok_loaded = sem("tok_loaded")
        ln_pe, ln_dve, ln_act = sem("ln_pe"), sem("ln_dve"), sem("ln_act")
        filt_sums, filt_copied_dve, filt_copied_act = sem("filt_sums"), sem("filt_copied_dve"), sem("filt_copied_act")
        filt_mixed = sem("filt_mixed")
        result_ready, out_stored = sem("result_ready"), sem("out_stored")

        block = ctx.enter_context(nc.Block())

        SCORE = 4
        FIN_PE, FIN_DVE, FIN_ACT = 3, 13, 1
        POST_PE, POST_DVE, POST_ACT = 6, 9, 8
        M_STEPS = 6
        LN_PE, LN_DVE, LN_ACT = 3, 6, 2
        MIX_CREDIT = 3
        NLOADS = 23
        CONSTS = 19
        DVE_SETUP = 24
        ACT_SETUP = 11
        ACT_FILT = 3
        PE_BC = 2 * TAPS + 2

        def conv_tile(g, c, t):
            return (g * 2 + c) * TILES + t

        def act_relus(g, c, t):
            done = conv_tile(g, c, t) * PARTS
            if isinstance(g, int) and g == 0:
                return done * ACT_SHARE[False]
            first = 2 * TILES * PARTS
            return done * ACT_SHARE[True] + first * (ACT_SHARE[False] - ACT_SHARE[True])

        def dve_relus(g, c, t):
            done = conv_tile(g, c, t) * PARTS
            if isinstance(g, int) and g == 0:
                return done * (SLOTS - ACT_SHARE[False])
            first = 2 * TILES * PARTS
            return done * (SLOTS - ACT_SHARE[True]) + first * (ACT_SHARE[True] - ACT_SHARE[False])

        def score_tile(g, c, t):
            return ((g - 1) * 2 + c) * TILES + t

        def taps_of(c, tap):
            src = xp if c == 0 else x2p
            return src[:, :, tap // 3:tap // 3 + H, tap % 3:tap % 3 + W]

        def slot(i):
            return ring[:, i % RING, :].rearrange("p (a h w) -> p a h w", a=PAIR, h=H)

        def weight(c, i, part, t):
            tap, grp = divmod(i, GROUPS)
            return nw[:, c, tap, bass.ds(t * PARTS + (ROWS * grp + part), 1)]

        def needed_quads(c_it, i):
            return c_it + (i - RING) // GROUPS + 1 + RING_CREDIT

        def interior(padded):
            return padded[:, :, 1:1 + H, 1:1 + W]

        def hw(v):
            return v.rearrange("p a (h w) -> p a h w", h=H)

        def diag(j):
            return ring[:, j, 0:HW]

        def weighed(j):
            return ring[:, j, HW:2 * HW]

        def spread(j):
            return misc if j % 2 == 0 else e_ps

        @block.sync
        def _(sp):
            def load(dst, src):
                sp.dma_start(dst, src).then_inc(loaded, 16)

            def column(v):
                return v.rearrange("(p o) -> p o", o=1)

            with nc.allow_non_contiguous_dma(reason="small transposed weights, once"):
                for c, name in enumerate(("L0_conv_w1", "L0_conv_w2")):
                    load(w_raw[c], a[name].rearrange("o i h w -> o (i h w)"))
                for name, src in (("g1", "bn1_gamma"), ("b1", "bn1_beta"), ("m1", "bn1_mean"), ("v1", "bn1_var"),
                                  ("g2", "bn2_gamma"), ("b2", "bn2_beta"), ("m2", "bn2_mean"), ("v2", "bn2_var"),
                                  ("fc2b", "fc2_b")):
                    load(col[name], column(a["L0_conv_" + src]))
                load(col["bh"], column(a["L1_attn_bh"]))
                load(col["wa"], a["L1_attn_Wa"])
                load(col["fc1b"][0:8, :], column(a["L0_conv_fc1_b"]))
                load(wt_sb, a["L1_attn_Wt"])
                load(wx_sb, a["L1_attn_Wx"])
                load(fc1T, a["L0_conv_fc1_w"].rearrange("r c -> c r"))
                load(fc2T[0:8, :], a["L0_conv_fc2_w"].rearrange("c r -> r c"))
                load(row[:, 0, 0:1], a["L1_attn_ba"].rearrange("(o p) -> o p", o=1))
                load(row[:, 1, :], a["L1_ffn_log_weights"].rearrange("(o p) -> o p", o=1))
                load(row[:, 2, :], a["L1_ffn_gumbel"].rearrange("(o p) -> o p", o=1))
                load(mu_raw, a["L1_ffn_M_u"].rearrange("i t d e -> d i t e"))
                load(xn.rearrange("p (n q) -> p n q", n=PAIR), x_dram[0])

            sp.wait_ge(act_setup, ACT_FILT)
            sp.dma_start(filt_dram, phiT).then_inc(filters_stored, 16)

            def next_pair(g):
                sp.wait_ge(x_padded, g)
                sp.dma_start(xn.rearrange("p (n q) -> p n q", n=PAIR),
                             x_dram[bass.ds(g, 1)].rearrange("o p n q -> (o p) n q")).then_inc(x_loaded, 16)

            def store_mid(g, c):
                sp.wait_ge(fin_dve, ((g - 1) * 2 + c + 1) * FIN_DVE)
                sp.dma_start(mid_dram[bass.ds((g - 1) * PAIR + c, 1)].rearrange("o p q -> (o p) q"),
                             tt[:, c, :]).then_inc(mid_stored, 16)

            if pairs > 1:
                next_pair(1)
            with sp.Fori(1, pairs) as g:
                store_mid(g, 0)
                store_mid(g, 1)
                sp.wait_ge(x_padded, g + 1)
                sp.dma_start(xn.rearrange("p (n q) -> p n q", n=PAIR),
                             x_dram[bass.ds((g + 1) % pairs, 1)].rearrange("o p n q -> (o p) n q")).then_inc(x_loaded, 16)
            store_mid(pairs, 0)
            store_mid(pairs, 1)

            sp.wait_ge(filters_stored, 16)
            sp.wait_ge(mid_stored, 16 * n_img)
            sp.wait_ge(fin_dve, n_img * FIN_DVE)
            sp.wait_ge(x_loaded, 16 * pairs)
            for kp in range(NK):
                if kp % 2 == 0:
                    k = kp // 2
                    if k >= 2:
                        sp.wait_ge(m_step, 1 + NLEN + (k - 1) * M_STEPS)
                    for sign, name in enumerate(("plus", "minus")):
                        sp.dma_start(raw[:, k % 2, sign], a["L1_ffn_M_phi_" + name][:, k].rearrange("i d e -> d i e"))\
                            .then_inc(m_loaded[k % 2], 16)
                src = bass.AP(tensor=filt, offset=kp * FROW, ap=[[1, P], [1, FW]])
                sp.dma_start(toep[:, kp, :], src).then_inc(toep_loaded, 16)
            sp.dma_start(tok, mid_dram[0]).then_inc(tok_loaded, 16)
            with sp.Fori(0, n_img) as b:
                sp.wait_ge(result_ready, b + 1)
                sp.dma_start(out_dram[bass.ds(b, 1)].rearrange("o p q -> (o p) q"), result).then_inc(out_stored, 16)
                sp.wait_ge(out_stored, (b + 1) * 16)
                sp.dma_start(tok, mid_dram[bass.ds((b + 1) % n_img, 1)].rearrange("o p q -> (o p) q")).then_inc(tok_loaded, 16)
            sp.wait_ge(out_stored, 16 * n_img)
            sp.wait_ge(tok_loaded, 16 * (n_img + 1))


        @block.gpsimd
        def _(pool):
            nc.gpsimd.memset(ring[:, 2, :], 0.0).then_inc(consts, 1)
            pool.wait_ge(consts, 1)
            with nc.allow_non_contiguous_dma(reason="filters transposed, once"):
                src = a["L1_ffn_phi"][0:HW, :].rearrange("(t two) k -> two k t", two=2)
                for par in range(2):
                    pool.dma_start(ring[par * NF:(par + 1) * NF, 2, P:P + HALF], src[par]).then_inc(filters_loaded, 16)
                    pool.dma_start(small[par * NF:(par + 1) * NF, 0:1],
                                   a["L1_ffn_sigma"].rearrange("(k o) -> k o", o=1)).then_inc(filters_loaded, 16)
            made = 1
            for buf, val in ((ident, 0.0), (sums, 1.0), (means, 1.0 / P), (nhalf, -0.5), (zeros, 0.0),
                             (ones_hot, 0.0), (wa_hot, 0.0), (ep, OUTSIDE), (xl[:, :, 0:1], 0.0),
                             (xl[:, :, EP - 1:EP], 0.0), (xp, 0.0), (x2p, 0.0)):
                nc.gpsimd.memset(buf, val).then_inc(consts, 1)
                made += 1
            for i in range(4):
                nc.gpsimd.memset(row[:, 7, i:i + 1], float(4 - i)).then_inc(consts, 1)
                made += 1
            pool.wait_ge(consts, made)
            nc.gpsimd.memset(ones_hot[:, ROWS - 1:ROWS], 1.0).then_inc(consts, 1)
            nc.gpsimd.affine_select(out=ident, in_=ident, compare_op=ALU.not_equal, fill=1.0, base=0,
                                    pattern=[[-1, P]], channel_multiplier=1).then_inc(consts, 1)
            made += 2
            assert made == CONSTS

            def boxes(conv_index, src, ready, count):
                s = Steps(box_step, 4, conv_index)
                pool.wait_ge(ready, count)
                pool.wait_ge(sums_closed, conv_index + 1)
                s.link(pool, nc.gpsimd.tensor_tensor(box_rows, src[:, :, :, 0:W], src[:, :, :, 1:1 + W], ALU.add))
                s.link(pool, nc.gpsimd.tensor_tensor(box_rows, box_rows, src[:, :, :, 2:2 + W], ALU.add))
                s.link(pool, nc.gpsimd.tensor_tensor(box, box_rows[:, :, 0:H, :], box_rows[:, :, 1:1 + H, :], ALU.add))
                s.did(nc.gpsimd.tensor_tensor(box, box, box_rows[:, :, 2:2 + H, :], ALU.add))

            with pool.Fori(0, pairs) as g:
                boxes(g * 2, xp, x_padded, g + 1)
                boxes(g * 2 + 1, x2p, x2_ready, g + 1)


        @block.scalar
        def _(act):
            s = Steps(act_setup, 11, 0)
            act.wait_ge(filters_loaded, 64)
            act.wait_ge(consts, CONSTS)
            act.wait_ge(loaded, 16 * NLOADS)
            s.link(act, nc.scalar.activation(sig, sig, ACT.Sqrt))
            s.link(act, nc.scalar.activation(sig, sig, ACT.Sqrt))
            s.did(nc.scalar.activation(ring[0:NK, 2, P:FROW], ring[0:NK, 2, P:FROW], ACT.Copy, scale=sig))
            act.wait_ge(dve_setup, 2)
            s.did(nc.scalar.activation(col["v1"], col["v1"], ACT.Sqrt))
            s.did(nc.scalar.activation(col["v2"], col["v2"], ACT.Sqrt))
            act.wait_ge(pe_setup, TAPS)
            s.did(nc.scalar.activation(nw[:, 0], acc[:, 0:TAPS * P].rearrange("p (t o) -> p t o", t=TAPS), ACT.Copy, scale=-1.0))
            act.wait_ge(pe_setup, 2 * TAPS)
            s.did(nc.scalar.activation(nw[:, 1], acc[:, 0:TAPS * P].rearrange("p (t o) -> p t o", t=TAPS), ACT.Copy, scale=-1.0))
            s.did(nc.scalar.activation(wa_hot[:, ROWS - 1:ROWS], col["wa"], ACT.Copy))
            s.did(nc.scalar.activation(col["fc2b"], col["fc2b"], ACT.Copy, scale=0.5))
            act.wait_ge(dve_setup, 5)
            s.did(nc.scalar.activation(row[:, 5, :], row[:, 4, :], ACT.Exp))
            s.did(nc.scalar.activation(interior(xp), xn.rearrange("p (a h w) -> p a h w", a=PAIR, h=H), ACT.Copy))
            assert s.n == 11
            act.wait_ge(act_setup, ACT_SETUP)
            act.wait_ge(dve_setup, DVE_SETUP)
            act.sem_inc(x_padded, 1)
            act.wait_ge(m_step, 1 + NLEN)
            act.wait_ge(filters_stored, 16)

            def loop(g, c, conv, scores):
                mine = act_slots(ACT_SHARE[scores])
                with act.Fori(0, TILES) as t:
                    if conv:
                        it0 = conv_tile(g, c, t) * (PARTS * ITER_QUADS)
                        act.wait_ge(relus_used, it0 + RING_CREDIT)
                        nc.scalar.activation(ones_now, ones_hot[:, bass.ds((ROWS - PARTS) - t * PARTS, ROWS + PARTS - 1)],
                                             ACT.Copy).then_inc(hot_ready, 1)
                    for part in range(PARTS):
                        order = []
                        for qd in range(TQUADS):
                            if scores:
                                order.append(("tanh", qd))
                            if conv:
                                lo, hi = qd * SLOTS // TQUADS, (qd + 1) * SLOTS // TQUADS
                                order += [("relu", i) for i in range(lo, hi) if i in mine]
                        for kind, i in order:
                            if kind == "relu":
                                act.wait_ge(relus_used, needed_quads(it0 + part * ITER_QUADS, i))
                                nc.scalar.activation(slot(i), taps_of(c, i // GROUPS), ACT.Relu,
                                                     bias=weight(c, i, part, t)).then_inc(relu_act, 1)
                            else:
                                r = part * TQUADS + i
                                act.wait_ge(tanhs_used, score_tile(g, c, t) * TILE_TQUADS + (r + 1))
                                for j in range(GROUPS):
                                    nc.scalar.activation(tring[:, (r % 2) * GROUPS + j, :], kT[:, c, :], ACT.Tanh,
                                                         bias=qT[:, c, bass.ds(t * P + (ROWS * j + r), 1)])\
                                        .then_inc(tanh_ready, 1)

            def finish(g, c):
                before = (g - 1) * 2 + c
                act.wait_ge(score_step, (before + 1) * (TILES * SCORE) + 1)
                nc.scalar.activation(expd, scores3, ACT.Exp).then_inc(fin_act, 1)

            def mid(g):
                act.wait_ge(sums_closed, g * 2 + 2)
                for n in range(PAIR):
                    nc.scalar.activation(interior(x2p)[:, n], acc[:, n * HW:(n + 1) * HW].rearrange("p (h w) -> p h w", h=H),
                                         ACT.Relu, bias=col["bi1"], scale=col["sc1"]).then_inc(post_act, 1)
                act.wait_ge(post_act, g * POST_ACT + 2)
                act.sem_inc(x2_ready, 1)

            def post(g):
                s = Steps(post_act, POST_ACT, g)
                s.n = 2
                dve, pe = Steps(post_dve, POST_DVE, g), Steps(post_pe, POST_PE, g)
                act.wait_ge(sums_closed, g * 2 + 3)
                for n in range(PAIR):
                    s.did(nc.scalar.activation(ring[:, 0, n * HW:(n + 1) * HW], acc[:, n * HW:(n + 1) * HW], ACT.Identity,
                                               bias=col["bi2"], scale=col["sc2"], accum_out=pooled[:, n:n + 1]))
                act.wait_ge(pe.sem, pe.at(1))
                s.did(nc.scalar.activation(z1, misc[0:8, 0:PAIR], ACT.Relu, bias=col["fc1b"][0:8, :], scale=1.0 / HW))
                act.wait_ge(pe.sem, pe.at(2))
                s.did(nc.scalar.activation(th, misc[:, BANK:BANK + PAIR], ACT.Tanh, bias=col["fc2b"], scale=0.5))
                act.wait_ge(dve.sem, dve.at(5))
                s.did(nc.scalar.activation(ring[:, 2, :], ring[:, 1, :], ACT.Square))
                act.wait_ge(pe.sem, pe.at(4))
                act.wait_ge(dve.sem, dve.at(6))
                s.did(nc.scalar.activation(ring[:, 3, :], ring[:, 3, :], ACT.Sqrt))
                assert s.n == POST_ACT
                act.wait_ge(pe.sem, pe.at(5))
                nc.scalar.activation(qT, acc[:, :].rearrange("p (a q) -> p a q", a=PAIR), ACT.Identity,
                                     bias=col["bh"]).then_inc(queries_ready, 1)

            def pad_next(g):
                act.wait_ge(post_dve, g * POST_DVE + 4)
                act.wait_ge(x_loaded, (g + 1) * 16)
                nc.scalar.activation(interior(xp), xn.rearrange("p (a h w) -> p a h w", a=PAIR, h=H), ACT.Copy)\
                    .then_inc(x_padded, 1)
                act.wait_ge(post_dve, (g + 1) * POST_DVE)
                act.wait_ge(queries_ready, g + 1)
                act.wait_ge(x_padded, g + 2)

            loop(0, 0, True, False)
            mid(0)
            loop(0, 1, True, False)
            post(0)
            pad_next(0)
            with act.Fori(1, pairs) as g:
                loop(g, 0, True, True)
                mid(g)
                finish(g, 0)
                act.wait_ge(fin_dve, ((g - 1) * 2 + 1) * FIN_DVE)
                loop(g, 1, True, True)
                finish(g, 1)
                act.wait_ge(fin_dve, ((g - 1) * 2 + 2) * FIN_DVE)
                post(g)
                pad_next(g)
            loop(pairs, 0, False, True)
            finish(pairs, 0)
            act.wait_ge(fin_dve, (n_img - 1) * FIN_DVE)
            loop(pairs, 1, False, True)
            finish(pairs, 1)

            with act.Fori(0, n_img) as b:
                dve, pe = Steps(ln_dve, LN_DVE, b), Steps(ln_pe, LN_PE, b)
                act.wait_ge(dve.sem, dve.at(1))
                nc.scalar.activation(ln_b, ln_a, ACT.Square).then_inc(ln_act, 1)
                act.wait_ge(dve.sem, dve.at(2))
                nc.scalar.activation(ln_b, ln_b, ACT.Sqrt).then_inc(ln_act, 1)
                for n in range(NK):
                    act.wait_ge(filt_sums, b * NK + (n + 1))
                    act.wait_ge(filt_mixed, b * NK + (n + 1))
                    nc.scalar.activation(conv_out[:, n % 3, 1, :], acc[:, (n % 2) * HW + HALF:(n % 2) * HW + HW],
                                         ACT.Copy).then_inc(filt_copied_act, 1)


        @block.vector
        def _(dve):
            v = nc.vector
            s = Steps(dve_setup, DVE_SETUP, 0)
            dve.wait_ge(loaded, 16 * NLOADS)
            dve.wait_ge(consts, CONSTS)
            s.did(v.tensor_scalar_add(col["v1"], col["v1"], BN_EPS))
            s.did(v.tensor_scalar_add(col["v2"], col["v2"], BN_EPS))
            s.link(dve, v.tensor_tensor(row[:, 3, :], row[:, 1, :], row[:, 2, :], ALU.add))
            s.link(dve, v.tensor_reduce(row[:, 0, 1:2], row[:, 3, :], AX.X, ALU.max))
            s.did(v.tensor_scalar(row[:, 4, :], row[:, 3, :], row[:, 0, 1:2], None, ALU.subtract))
            dve.wait_ge(act_setup, 10)
            s.link(dve, v.tensor_reduce(row[:, 0, 2:3], row[:, 5, :], AX.X, ALU.add))
            s.link(dve, v.reciprocal(row[:, 0, 2:3], row[:, 0, 2:3]))
            s.link(dve, v.tensor_scalar(row[:, 5, :], row[:, 5, :], row[:, 0, 2:3], None, ALU.mult))
            s.link(dve, v.tensor_reduce(row[:, 0, 3:4], row[:, 5, :], AX.X, ALU.max))
            s.link(dve, v.scalar_tensor_tensor(row[:, 6, :], row[:, 5, :], row[:, 0, 3:4], row[:, 7, :], ALU.is_equal, ALU.mult))
            s.link(dve, v.tensor_reduce(row[:, 0, 3:4], row[:, 6, :], AX.X, ALU.max))
            s.link(dve, v.tensor_scalar(row[:, 6, :], row[:, 6, :], row[:, 0, 3:4], None, ALU.is_equal))
            s.link(dve, v.tensor_tensor(row[:, 6, :], row[:, 6, :], row[:, 5, :], ALU.subtract))
            s.did(v.tensor_tensor(row[:, 6, :], row[:, 6, :], row[:, 5, :], ALU.add))
            for c in (0, 1):
                g_, b_, m_, v_ = (col[n + "12"[c]] for n in ("g", "b", "m", "v"))
                sc, bi = col[("sc1", "sc2")[c]], col[("bi1", "bi2")[c]]
                s.link(dve, v.reciprocal(v_, v_))
                v.tensor_reduce(col["sw"], w_raw[c], AX.X, ALU.add)
                s.link(dve, v.tensor_tensor(v_, v_, g_, ALU.mult))
                v.tensor_scalar(sc, v_, -2.0, None, ALU.mult)
                s.link(dve, v.tensor_tensor(m_, m_, col["sw"], ALU.add))
                s.link(dve, v.tensor_tensor(m_, m_, v_, ALU.mult))
                if c == 0:
                    s.link(dve, v.tensor_tensor(bi, b_, m_, ALU.subtract))
                else:
                    s.link(dve, v.tensor_tensor(bi, b_, m_, ALU.subtract))
            assert s.n == DVE_SETUP, s.n
            dve.wait_ge(pe_setup, PE_BC)
            v.tensor_copy(col["ba"], misc[:, 0:1])
            v.tensor_copy(wlen, misc[:, BANK:BANK + NLEN]).then_inc(m_step, 1)
            dve.wait_ge(m_step, 1)
            for r in range(NLEN):
                if r == 0:
                    i = v.tensor_scalar(mu[:, :, 0, :], mu_raw[:, 0], wlen[:, 0:1], None, ALU.mult)
                else:
                    i = v.scalar_tensor_tensor(mu[:, :, r, :], mu_raw[:, r], wlen[:, r:r + 1], mu[:, :, r - 1, :], ALU.mult, ALU.add)
                i.then_inc(m_step, 1)
                dve.wait_ge(m_step, 2 + r)
            dve.wait_ge(filters_stored, 16)
            dve.wait_ge(act_setup, 11)

            def score(g, c, t):
                s = Steps(score_step, SCORE, score_tile(g, c, t), 1)
                dve.wait_ge(tanhs_used, (score_tile(g, c, t) + 1) * TILE_TQUADS + 2)
                s.link(dve, v.tensor_scalar(ep[:, 1:1 + HW], e_ps[:, :], col["ba"], None, ALU.add, ALU.max, accum_out=m_cur))
                for j in range(3):
                    last = v.tensor_tensor(prod[:, j, :], ep[:, bass.ds(t * P + j, P)], ident, ALU.mult)
                s.link(dve, last)
                s.link(dve, v.tensor_reduce(e_cur, prod, AX.X, ALU.add))
                s.link(dve, v.tensor_scalar(scores3[:, bass.ds(t, 1), :].rearrange("p o j -> p (o j)"), e_cur, m_cur, None, ALU.subtract))

            def relus(g, c, t, parts, scores, late=None):
                mine = act_slots(ACT_SHARE[scores])
                it0 = conv_tile(g, c, t) * (PARTS * ITER_QUADS)
                for part in parts:
                    last = None
                    for i in range(SLOTS):
                        if late is not None and part == 0 and i == RING + 2:
                            late()
                        if i in mine:
                            continue
                        if last != (i - RING) // GROUPS:
                            last = (i - RING) // GROUPS
                            dve.wait_ge(relus_used, needed_quads(it0 + part * ITER_QUADS, i))
                        v.tensor_scalar(slot(i), taps_of(c, i // GROUPS), weight(c, i, part, t), 0.0,
                                        ALU.add, ALU.max).then_inc(relu_dve, 1)

            def loop(g, c, conv, scores):
                if not scores:
                    with dve.Fori(0, TILES) as t:
                        relus(g, c, t, range(PARTS), scores)
                elif conv:
                    relus(g, c, 0, range(PARTS), scores)
                    with dve.Fori(1, TILES) as t:
                        relus(g, c, t, range(PARTS), scores, late=lambda: score(g, c, t - 1))
                    score(g, c, TILES - 1)
                else:
                    with dve.Fori(0, TILES) as t:
                        score(g, c, t)

            def finish(g, c):
                before = (g - 1) * 2 + c
                s = Steps(fin_dve, FIN_DVE, before)
                dve.wait_ge(fin_act, before + 1)
                s.link(dve, v.tensor_reduce(s8, expd, AX.X, ALU.add))
                s.link(dve, v.tensor_scalar_add(s8, s8, ATTN_EPS))
                s.link(dve, v.reciprocal(r8, s8))
                s.link(dve, v.tensor_tensor(probs, expd, r8.rearrange("p (t o) -> p t o", o=1).broadcast_to([P, TILES, 3]), ALU.mult))
                for j in range(3):
                    s.did(v.tensor_tensor(diag(j).rearrange("p (t q) -> p t q", t=TILES),
                                          ident.rearrange("p (o q) -> p o q", o=1).broadcast_to([P, TILES, P]),
                                          probs[:, :, j:j + 1].broadcast_to([P, TILES, P]), ALU.mult))
                for j in range(3):
                    dve.wait_ge(fin_pe, before * FIN_PE + j + 1)
                    s.link(dve, v.tensor_tensor(weighed(j), spread(j)[:, :], xl[:, c, j:j + HW], ALU.mult))
                for j in range(3):
                    s.link(dve, v.tensor_tensor(tt[:, c, :], tt[:, c, :], weighed(j), ALU.add))
                assert s.n == FIN_DVE, s.n

            def post(g):
                s = Steps(post_dve, POST_DVE, g)
                actor, pe = Steps(post_act, POST_ACT, g), Steps(post_pe, POST_PE, g)
                dve.wait_ge(actor.sem, actor.at(6))
                s.link(dve, v.tensor_scalar(gate, th, 0.5, 0.5, ALU.mult, ALU.add))
                if not (isinstance(g, int) and g == 0):
                    dve.wait_ge(mid_stored, g * (16 * PAIR))
                for n in range(PAIR):
                    s.did(v.scalar_tensor_tensor(hw(tt)[:, n], ring[:, 0, n * HW:(n + 1) * HW].rearrange("p (h w) -> p h w", h=H),
                                                 gate[:, n:n + 1], interior(xp)[:, n], ALU.mult, ALU.add))
                dve.wait_ge(post_dve, s.at(3))
                s.did(v.tensor_scalar(tt, tt, 0.0, None, ALU.max))
                dve.wait_ge(pe.sem, pe.at(3))
                s.did(v.tensor_tensor(ring[:, 1, :], tt.rearrange("p a q -> p (a q)"), acc[:, :], ALU.subtract))
                dve.wait_ge(pe.sem, pe.at(4))
                s.did(v.tensor_scalar_add(ring[:, 3, :], acc[:, :], LN_EPS))
                dve.wait_ge(actor.sem, actor.at(8))
                s.link(dve, v.reciprocal(ring[:, 4, :], ring[:, 3, :]))
                s.did(v.tensor_tensor(xl[:, :, 1:1 + HW], ring[:, 1, :].rearrange("p (a q) -> p a q", a=PAIR),
                                      ring[:, 4, :].rearrange("p (a q) -> p a q", a=PAIR), ALU.mult))
                dve.wait_ge(pe.sem, pe.at(6))
                v.tensor_copy(kT[:, 0, :], misc[:, :])
                s.did(v.tensor_copy(kT[:, 1, :], e_ps[:, :]))
                assert s.n == POST_DVE

            dve.sem_inc(score_step, 1)
            for c in (0, 1):
                if c == 0:
                    dve.wait_ge(x_padded, 1)
                else:
                    dve.wait_ge(x2_ready, 1)
                loop(0, c, True, False)
            post(0)
            dve.wait_ge(x_padded, 2)
            with dve.Fori(1, pairs) as g:
                loop(g, 0, True, True)
                finish(g, 0)
                dve.wait_ge(x2_ready, g + 1)
                loop(g, 1, True, True)
                finish(g, 1)
                post(g)
                dve.wait_ge(x_padded, g + 2)
            loop(pairs, 0, False, True)
            finish(pairs, 0)
            loop(pairs, 1, False, True)
            finish(pairs, 1)

            for k in range(NF):
                s = Steps(m_step, M_STEPS, k, 1 + NLEN)
                dve.wait_ge(m_loaded[k % 2], 32 * (k // 2 + 1))
                s.did(v.tensor_tensor(xm[:, 0], raw[:, k % 2, 0], raw[:, k % 2, 1], ALU.add))
                s.link(dve, v.tensor_tensor(xm[:, 1], raw[:, k % 2, 0], raw[:, k % 2, 1], ALU.subtract))
                s.link(dve, v.tensor_scalar(mf[:, k, :, 0, :], xm[:, :, 0, :], wlen[:, 0:1], None, ALU.mult))
                for r in range(1, NLEN):
                    s.link(dve, v.scalar_tensor_tensor(mf[:, k, :, r, :], xm[:, :, r, :], wlen[:, r:r + 1], mf[:, k, :, r - 1, :], ALU.mult, ALU.add))
            v.memset(uT[:, :, 0:1], 0.0)
            with dve.Fori(0, n_img) as b:
                s = Steps(ln_dve, LN_DVE, b)
                actor, pe = Steps(ln_act, LN_ACT, b), Steps(ln_pe, LN_PE, b)
                dve.wait_ge(pe.sem, pe.at(1))
                s.did(v.tensor_tensor(ln_a, tok, e_ps[:, :], ALU.subtract))
                dve.wait_ge(pe.sem, pe.at(2))
                s.did(v.tensor_scalar_add(ln_b, e_ps[:, :], LN_EPS))
                dve.wait_ge(actor.sem, actor.at(2))
                s.link(dve, v.reciprocal(ln_b, ln_b))
                s.did(v.tensor_tensor(uT[:, :, 1:FW].rearrange("p a t -> p t a"),
                                      ln_a.rearrange("p (t a) -> p t a", a=2), ln_b.rearrange("p (t a) -> p t a", a=2), ALU.mult))
                dve.wait_ge(s.sem, s.at(4))
                s.did(v.tensor_copy(uR, uT[:, :, HALF:0:-1]))
                dve.wait_ge(pe.sem, pe.at(3))
                s.did(v.tensor_copy(u.rearrange("p a i d -> p (a i d)"), e_ps[:, :]))
                for n in range(NK):
                    dve.wait_ge(filt_sums, b * NK + (n + 1))
                    dve.wait_ge(filt_mixed, b * NK + (n + 1))
                    v.tensor_copy(conv_out[:, n % 3, 0, :], acc[:, (n % 2) * HW:(n % 2) * HW + HALF]).then_inc(filt_copied_dve, 1)
                dve.wait_ge(filt_mixed, b * NK + (NK + MIX_CREDIT))
                v.tensor_tensor(result.rearrange("p (t a) -> p t a", a=2), tok.rearrange("p (t a) -> p t a", a=2),
                                misc[:, :].rearrange("p (a t) -> p t a", a=2), ALU.add).then_inc(result_ready, 1)
                assert s.n == LN_DVE

        @block.tensor
        def _(pe):
            mm = nc.tensor.matmul
            zb = zeros[:, :].bitcast(BF16)

            def open_sums(ps, banks):
                for k in range(banks):
                    mm(ps[:, k * BANK:(k + 1) * BANK], zb[:, 0:P], zb[:, 0:BANK], start=True, stop=False, skip_group_check=True)

            pe.wait_ge(loaded, 16 * NLOADS)
            pe.wait_ge(consts, CONSTS)
            for c in (0, 1):
                if c:
                    pe.wait_ge(act_setup, 6)
                w_by_tap = w_raw[c].rearrange("p (i t) -> p t i", t=TAPS)
                for tap in range(TAPS):
                    nc.tensor.transpose(acc[:, tap * P:(tap + 1) * P], w_by_tap[:, tap, :], ident).then_inc(pe_setup, 1)
            mm(misc[:, 0:1], sums[0:1, :], row[:, 0, 0:1], start=True, stop=True).then_inc(pe_setup, 1)
            pe.wait_ge(dve_setup, 14)
            mm(misc[:, BANK:BANK + NLEN], sums[0:1, :], row[:, 6, :], start=True, stop=True).then_inc(pe_setup, 1)
            pe.wait_ge(act_setup, 11)
            pe.sem_inc(relus_used, RING_CREDIT)
            pe.sem_inc(tanhs_used, 2)
            pe.sem_inc(sums_closed, 1)
            pe.sem_inc(filt_mixed, MIX_CREDIT)
            pe.wait_ge(dve_setup, DVE_SETUP)

            def loop(g, c, conv, scores):
                mine = act_slots(ACT_SHARE[scores])
                if conv:
                    open_sums(acc, PAIRPOS // BANK)
                with pe.Fori(0, TILES) as t:
                    if conv:
                        it0 = conv_tile(g, c, t) * PARTS
                        pe.wait_ge(hot_ready, conv_tile(g, c, t) + 1)
                    for part in range(PARTS):
                        order = []
                        for q in range(TAPS):
                            if conv:
                                order.append(("relu", q))
                            if scores and q >= 1:
                                order.append(("tanh", q - 1))
                        for kind, q in order:
                            if kind == "relu":
                                n_act = sum(i in mine for i in range(GROUPS * (q + 1)))
                                n_dve = GROUPS * (q + 1) - n_act
                                per_act, per_dve = len(mine), SLOTS - len(mine)
                                here = [i in mine for i in range(GROUPS * q, GROUPS * (q + 1))]
                                if any(here):
                                    pe.wait_ge(relu_act, act_relus(g, c, t) + (part * per_act + n_act))
                                if not all(here):
                                    pe.wait_ge(relu_dve, dve_relus(g, c, t) + (part * per_dve + n_dve))
                                hot = ones_now[:, PARTS - 1 - part:PARTS - 1 - part + ROWS]
                                for k in range(PAIRPOS // BANK):
                                    for grp in range(GROUPS):
                                        last = mm(acc[ROWS * grp:ROWS * (grp + 1), k * BANK:(k + 1) * BANK], hot,
                                                  ring[:, (GROUPS * q + grp) % RING, k * BANK:(k + 1) * BANK],
                                                  start=False, stop=False, skip_group_check=True)
                                last.then_inc(relus_used, 1)
                            else:
                                r = part * TQUADS + q
                                if r == 0:
                                    pe.wait_ge(score_step, score_tile(g, c, t) * SCORE + 1)
                                    open_sums(e_ps, HW // BANK)
                                pe.wait_ge(tanh_ready, score_tile(g, c, t) * (TILE_TQUADS * GROUPS) + GROUPS * (r + 1))
                                hot = wa_hot[:, ROWS - 1 - r:2 * ROWS - 1 - r]
                                for k in range(HW // BANK):
                                    for j in range(GROUPS):
                                        last = mm(e_ps[ROWS * j:ROWS * (j + 1), k * BANK:(k + 1) * BANK], hot,
                                                  tring[:, (r % 2) * GROUPS + j, k * BANK:(k + 1) * BANK],
                                                  start=False, stop=False, skip_group_check=True)
                                last.then_inc(tanhs_used, 1)

            def close_sums(g, c):
                pe.wait_ge(box_step, ((g * 2 + c) + 1) * 4)
                for k in range(PAIRPOS // BANK):
                    rows = BANK // W
                    last = mm(acc[:, k * BANK:(k + 1) * BANK], nhalf,
                              box[:, k * rows // H, (k * rows) % H:(k * rows) % H + rows, :],
                              start=False, stop=True, skip_group_check=True)
                last.then_inc(sums_closed, 1)

            def finish(g, c):
                before = (g - 1) * 2 + c
                for j in range(3):
                    pe.wait_ge(fin_dve, before * FIN_DVE + (5 + j if j < 2 else 8))
                    for k in range(HW // BANK):
                        last = mm(spread(j)[:, k * BANK:(k + 1) * BANK], sums, diag(j)[:, k * BANK:(k + 1) * BANK],
                                  start=True, stop=True)
                    last.then_inc(fin_pe, 1)
                pe.wait_ge(fin_dve, (before + 1) * FIN_DVE)

            def post(g):
                s = Steps(post_pe, POST_PE, g)
                actor, dve = Steps(post_act, POST_ACT, g), Steps(post_dve, POST_DVE, g)
                pe.wait_ge(actor.sem, actor.at(4))
                s.did(mm(misc[0:8, 0:PAIR], fc1T, pooled, start=True, stop=True))
                pe.wait_ge(actor.sem, actor.at(5))
                s.did(mm(misc[:, BANK:BANK + PAIR], fc2T[0:8, :], z1, start=True, stop=True))
                t2 = tt.rearrange("p a q -> p (a q)")

                def wide(stationary, moving, targets):
                    for k, o in enumerate(targets):
                        last = mm(o, stationary, moving[k], start=True, stop=True)
                    return last

                acc_banks = [acc[:, k * BANK:(k + 1) * BANK] for k in range(PAIRPOS // BANK)]
                pe.wait_ge(dve.sem, dve.at(4))
                s.did(wide(means, [t2[:, k * BANK:(k + 1) * BANK] for k in range(4)], acc_banks))
                pe.wait_ge(actor.sem, actor.at(7))
                s.did(wide(means, [ring[:, 2, k * BANK:(k + 1) * BANK] for k in range(4)], acc_banks))
                pe.wait_ge(dve.sem, dve.at(8))
                tokens = [xl[:, n, 1 + k * BANK:1 + (k + 1) * BANK] for n in range(PAIR) for k in range(HW // BANK)]
                s.did(wide(wt_sb, tokens, acc_banks))
                s.did(wide(wx_sb, tokens, [p[:, k * BANK:(k + 1) * BANK] for p in (misc, e_ps) for k in range(HW // BANK)]))
                pe.wait_ge(queries_ready, g + 1)
                pe.wait_ge(dve.sem, dve.at(9))

            loop(0, 0, True, False)
            close_sums(0, 0)
            pe.wait_ge(x2_ready, 1)
            loop(0, 1, True, False)
            close_sums(0, 1)
            post(0)
            with pe.Fori(1, pairs) as g:
                loop(g, 0, True, True)
                close_sums(g, 0)
                finish(g, 0)
                pe.wait_ge(x2_ready, g + 1)
                loop(g, 1, True, True)
                close_sums(g, 1)
                finish(g, 1)
                post(g)
            loop(pairs, 0, False, True)
            finish(pairs, 0)
            loop(pairs, 1, False, True)
            finish(pairs, 1)

            pe.wait_ge(toep_loaded, 16 * NK)
            pe.wait_ge(m_step, 1 + NLEN + NF * M_STEPS)
            with pe.Fori(0, n_img) as b:
                s = Steps(ln_pe, LN_PE, b)
                actor, dve = Steps(ln_act, LN_ACT, b), Steps(ln_dve, LN_DVE, b)
                pe.wait_ge(tok_loaded, (b + 1) * 16)
                for k in range(HW // BANK):
                    last = mm(e_ps[:, k * BANK:(k + 1) * BANK], means, tok[:, k * BANK:(k + 1) * BANK], start=True, stop=True)
                s.did(last)
                pe.wait_ge(actor.sem, actor.at(1))
                for k in range(HW // BANK):
                    last = mm(e_ps[:, k * BANK:(k + 1) * BANK], means, ln_b[:, k * BANK:(k + 1) * BANK], start=True, stop=True)
                s.did(last)
                pe.wait_ge(dve.sem, dve.at(5))
                for par in range(2):
                    for i in range(TB):
                        last = nc.tensor.transpose(e_ps[:, (par * TB + i) * P:(par * TB + i + 1) * P],
                                                   uR[:, par, (TB - 1 - i) * P:(TB - i) * P], ident)
                s.did(last)
                for par in range(2):
                    for tap in range(3):
                        src, back = (par - tap) % 2, (tap + 1 - par) // 2
                        for r, (lo, hi) in enumerate(SEGS):
                            mm(misc[:, par * HALF + lo:par * HALF + hi], mu[:, tap, r, :], uT[:, src, 1 + lo - back:1 + hi - back],
                               start=(tap == 0 and r == 0), stop=False, skip_group_check=True)
                pe.wait_ge(dve.sem, dve.at(6))

                def filter_sums(n):
                    k, odd = divmod(n, 2)
                    f = toep[:, odd * NF + k, :]
                    o0 = (n % 2) * HW
                    if n >= 2:
                        pe.wait_ge(filt_copied_dve, b * NK + (n - 1))
                        pe.wait_ge(filt_copied_act, b * NK + (n - 1))
                    for par in range(2):
                        src = par ^ odd
                        lead = 0 if (odd and par == 0) else 1
                        for i in range(TB):
                            last = mm(acc[:, o0 + par * HALF + i * P:o0 + (par + 1) * HALF], u[:, src, i, :],
                                      f[:, lead:lead + HALF - i * P], start=(i == 0), stop=(i == TB - 1), skip_group_check=True)
                    last.then_inc(filt_sums, 1)

                def mix(n):
                    k, odd = divmod(n, 2)
                    pe.wait_ge(filt_copied_dve, b * NK + (n + 1))
                    pe.wait_ge(filt_copied_act, b * NK + (n + 1))
                    for par in range(2):
                        for r, (lo, hi) in enumerate(SEGS):
                            last = mm(misc[:, par * HALF + lo:par * HALF + hi], mf[:, k, odd, r, :], conv_out[:, n % 3, par, lo:hi],
                                      start=False, stop=(n == NK - 1), skip_group_check=True)
                    last.then_inc(filt_mixed, 1)

                for n in range(NK):
                    filter_sums(n)
                    if n:
                        mix(n - 1)
                mix(NK - 1)


_NAMES = ["x", "L0_conv_w1", "L0_conv_bn1_gamma", "L0_conv_bn1_beta", "L0_conv_bn1_mean", "L0_conv_bn1_var",
          "L0_conv_w2", "L0_conv_bn2_gamma", "L0_conv_bn2_beta", "L0_conv_bn2_mean", "L0_conv_bn2_var",
          "L0_conv_fc1_w", "L0_conv_fc1_b", "L0_conv_fc2_w", "L0_conv_fc2_b", "L1_attn_Wt", "L1_attn_Wx",
          "L1_attn_Wa", "L1_attn_bh", "L1_attn_ba", "L1_ffn_sigma", "L1_ffn_phi", "L1_ffn_M_u",
          "L1_ffn_M_phi_plus", "L1_ffn_M_phi_minus", "L1_ffn_log_weights", "L1_ffn_gumbel"]


def kernel(**inputs):
    import numpy as np
    import concourse.bacc as bacc
    from concourse.bass_utils import run_bass_kernel_spmd

    nc = bacc.Bacc("TRN2", target_bir_lowering=False, num_devices=1)
    arrays, aps = {}, {}
    for name in _NAMES:
        arr = np.ascontiguousarray(inputs[name])
        arrays["in_" + name] = arr
        aps[name] = nc.dram_tensor("in_" + name, arr.shape, mybir.dt.from_np(arr.dtype), kind="ExternalInput").ap()
    out = nc.dram_tensor("out", arrays["in_x"].shape, FP32, kind="ExternalOutput").ap()
    build(nc, aps, out)
    r = run_bass_kernel_spmd(nc, [arrays], core_ids=[0])
    return r.results[0]["out"]
```

```python
import concourse.bass as bass
from concourse import mybir
from contextlib import ExitStack

FP32 = mybir.dt.float32
BF16 = mybir.dt.bfloat16
ALU = mybir.AluOpType
ACT = mybir.ActivationFunctionType
AX = mybir.AxisListType

P = 128
H = W = 32
HW = H * W
PW = W + 2
PAIR = 2
PAIRPOS = PAIR * HW
TAPS = 9
GROUPS = 4
ROWS = P // GROUPS
PARTS = 4
TILES = ROWS // PARTS
QUADS = 8
SLOTS = QUADS * GROUPS
RING = 8
RING_CREDIT = 2
MERGED = [(0,), (2,), (4,), (6,)]
TQUADS = 8
TILE_TQUADS = PARTS * TQUADS
TRING = 8
BANK = 512
BN_EPS = 1e-5
LN_EPS = 1e-5
ATTN_EPS = 1e-8
OUTSIDE = -1e30
EP = HW + 2
NF = 16
HALF = HW // 2
TB = HALF // P
FW = HALF + 1
NK = 2 * NF
NLEN = 4
SEGS = [(HALF // 2, HALF), (HALF // 4, HALF // 2), (HALF // 8, HALF // 4), (0, HALF // 8)]
ACT_TILES = {
    False: [GROUPS * q + (q // 2 + j) % GROUPS for q in range(QUADS) for j in (1, 3)[:2 - q % 4 // 3]],
    True: [GROUPS * q + (q // 2 + 2) % GROUPS for q in (0, 1, 2, 4, 5, 6)],
}


def taps_by_quad(grp):
    taps, out = iter(range(TAPS)), []
    for q in range(QUADS):
        out.append([next(taps) for _ in range(1 + (q in MERGED[grp]))])
    return out


QUAD_TAPS = [taps_by_quad(grp) for grp in range(GROUPS)]
SECOND_TAPS = [[t[1] for t in QUAD_TAPS[grp] if len(t) == 2] for grp in range(GROUPS)]


def dve_order(scores):
    out = []
    for q in range(QUADS):
        tiles = [i for i in range(GROUPS * q, GROUPS * (q + 1)) if i not in ACT_TILES[scores]]
        seconds = [i for i in tiles if q in MERGED[i % GROUPS]]
        out.append([(i, 0) for i in seconds] + [(i, 0) for i in tiles if i not in seconds] + [(i, 1) for i in seconds])
    return out


DVE_SHARE = {scores: sum(map(len, dve_order(scores))) for scores in (False, True)}
ACT_SHARE = {scores: len(ACT_TILES[scores]) for scores in (False, True)}


class Steps:

    def __init__(self, sem, per, before, offset=0):
        self.sem, self.per, self.base, self.n = sem, per, before * per + offset, 0

    def did(self, instruction):
        instruction.then_inc(self.sem, 1)
        self.n += 1
        assert self.n <= self.per

    def at(self, n):
        return self.base + n

    def link(self, engine, instruction):
        self.did(instruction)
        engine.wait_ge(self.sem, self.base + self.n)


def build(nc, a, out):
    n_img = a["x"].shape[0]
    pairs = n_img // PAIR
    x_dram = a["x"].rearrange("(g n) c h w -> g c n (h w)", n=PAIR)
    out_dram = out.rearrange("n c h w -> n c (h w)")
    mid_dram = nc.dram_tensor("tokens_after_attention", [n_img, P, HW], FP32, kind="Internal").ap()
    FROW = P + HALF
    filt = nc.dram_tensor("padded_filters", [NK, FROW], FP32, kind="Internal")
    filt_dram = filt.ap()

    with ExitStack() as ctx:
        def sem(name):
            return ctx.enter_context(nc.semaphore(name))

        arena = ctx.enter_context(nc.sbuf_tensor("arena", [P, 53100], FP32))
        place = {"at": 0, "top": 0}

        def take(*shape):
            size = 1
            for s in shape:
                size *= s
            o = place["at"]
            place["at"] += size
            assert place["at"] <= 53100, place
            v = arena[:, o:o + size]
            if len(shape) == 1:
                return v
            names = "abcd"[:len(shape)]
            return v.rearrange("p (%s) -> p %s" % (" ".join(names), " ".join(names)),
                               **{n: s for n, s in zip(names[1:], shape[1:])})

        ident = take(P)
        sums = take(P)
        means = take(P)
        nhalf = take(P)
        zeros = take(BANK)
        wlen = take(NLEN)
        mu = take(3, NLEN, P)
        small = take(64)
        kept = place["at"]
        ring = take(RING, PAIRPOS)
        tring = take(TRING, HW)
        xp = take(PAIR, PW, PW)
        x2p = take(PAIR, PW, PW)
        xn = take(PAIRPOS)
        box_rows = take(PAIR, PW, W)
        box = take(PAIR, H, W)
        nw = take(2, TAPS, P)
        pw = take(2, 1, P)
        kT = take(PAIR, HW)
        qT = take(PAIR, HW)
        xl = take(PAIR, EP)
        tt = take(PAIR, HW)
        ep = take(EP)
        prod = take(3, P)
        ones_hot = take(2 * ROWS - 1)
        wa_hot = take(2 * ROWS - 1)
        ones_now = take(ROWS + PARTS - 1)
        wt_sb, wx_sb = take(P), take(P)
        fc1T, fc2T = take(8), take(P)
        colv = take(24)
        scores3 = take(TILES, 3)
        expd = take(TILES, 3)
        probs = take(TILES, 3)
        place["at"] = kept
        toep = take(NK, FW)
        mf = take(NF, 2, NLEN, P)
        raw = take(2, 2, NLEN, P)
        xm = take(2, NLEN, P)
        tok = take(HW)
        uT = take(2, FW)
        uR = take(2, HALF)
        u = take(2, TB, P)
        conv_out = take(3, 2, HALF)
        ln_a, ln_b = take(HW), take(HW)
        result, residual = take(HW), take(HW)
        w_raw = [ring[:, c, 0:TAPS * P] for c in (0, 1)]
        phiT = ring[0:NK, 2, 0:FROW]
        mu_raw = ring[:, 3, 0:NLEN * 3 * P].rearrange("p (i t e) -> p i t e", i=NLEN, t=3)
        sig = small[0:NK, 0:1]
        row = small[0:1, 8:40].rearrange("p (a b) -> p a b", b=4)
        m_cur, e_cur = small[:, 40:41], small[:, 41:44]
        s8, r8 = small[:, 44:52], small[:, 52:60]
        col = {n: colv[:, i:i + 1] for i, n in enumerate(
            ["g1", "b1", "m1", "v1", "g2", "b2", "m2", "v2", "fc2b", "bh", "wa", "ba", "sc1", "bi1",
             "sc2", "bi2", "sw", "fc1b", "tmp"])}
        pooled, z1, gate, th = small[:, 60:62], small[0:8, 62:64], colv[:, 19:21], colv[:, 21:23]

        acc = ctx.enter_context(nc.psum_tensor("acc", [P, PAIRPOS], FP32))
        e_ps = ctx.enter_context(nc.psum_tensor("e_ps", [P, HW], FP32))
        misc = ctx.enter_context(nc.psum_tensor("misc", [P, HW], FP32))

        loaded = sem("loaded")
        consts = sem("consts")
        pe_setup, dve_setup, act_setup = sem("pe_setup"), sem("dve_setup"), sem("act_setup")
        filters_stored = sem("filters_stored")
        x_loaded, x_padded, queries_ready = sem("x_loaded"), sem("x_padded"), sem("queries_ready")
        filters_loaded = sem("filters_loaded")
        relu_dve, relu_act, relus_used = sem("relu_dve"), sem("relu_act"), sem("relu_quads_used")
        hot_ready = sem("hot_ready")
        tanh_ready, tanhs_used = sem("tanh_ready"), sem("tanh_quads_used")
        score_step = sem("score_step")
        box_step = sem("box_step")
        sums_closed = sem("sums_closed")
        x2_ready = sem("x2_ready")
        fin_pe, fin_dve, fin_act = sem("finish_pe"), sem("finish_dve"), sem("finish_act")
        post_pe, post_dve, post_act = sem("post_pe"), sem("post_dve"), sem("post_act")
        mid_stored = sem("mid_stored")
        toep_loaded = sem("toeplitz_loaded")
        m_loaded, m_step = [sem("m_loaded0"), sem("m_loaded1")], sem("m_step")
        tok_loaded = sem("tok_loaded")
        ln_pe, ln_dve, ln_act = sem("ln_pe"), sem("ln_dve"), sem("ln_act")
        filt_sums, filt_copied_dve, filt_copied_act = sem("filt_sums"), sem("filt_copied_dve"), sem("filt_copied_act")
        filt_mixed = sem("filt_mixed")
        residual_kept = sem("residual_kept")
        result_ready, out_stored = sem("result_ready"), sem("out_stored")

        block = ctx.enter_context(nc.Block())

        SCORE = 4
        FIN_PE, FIN_DVE, FIN_ACT = 3, 13, 1
        POST_PE, POST_DVE, POST_ACT = 6, 9, 8
        M_STEPS = 6
        LN_PE, LN_DVE, LN_ACT = 3, 6, 2
        AT_MEAN, AT_CENTRE, AT_SQUARE, AT_VAR, AT_EPS, AT_ROOT, AT_SCALE, AT_TRANSPOSE = 3, 4, 5, 7, 8, 9, 10, 14
        MIX_CREDIT = 3
        NLOADS = 23
        CONSTS = 19
        DVE_SETUP = 28
        ACT_SETUP = 11
        ACT_FILT = 3
        PE_BC = 2 * TAPS + 2

        def conv_tile(g, c, t):
            return (g * 2 + c) * TILES + t

        def act_relus(g, c, t):
            done = conv_tile(g, c, t) * PARTS
            if isinstance(g, int) and g == 0:
                return done * ACT_SHARE[False]
            first = 2 * TILES * PARTS
            return done * ACT_SHARE[True] + first * (ACT_SHARE[False] - ACT_SHARE[True])

        def dve_relus(g, c, t):
            done = conv_tile(g, c, t) * PARTS
            if isinstance(g, int) and g == 0:
                return done * DVE_SHARE[False]
            first = 2 * TILES * PARTS
            return done * DVE_SHARE[True] - first * (DVE_SHARE[True] - DVE_SHARE[False])

        def score_tile(g, c, t):
            return ((g - 1) * 2 + c) * TILES + t

        def taps_of(c, tap):
            src = xp if c == 0 else x2p
            return src[:, :, tap // 3:tap // 3 + H, tap % 3:tap % 3 + W]

        def buffer(part, i):
            return ring[:, (part * SLOTS + i) % RING, :]

        def tile(part, i):
            return buffer(part, i).rearrange("p (a h w) -> p a h w", a=PAIR, h=H)

        def weight(c, i, part, t, second=False):
            quad, grp = divmod(i, GROUPS)
            channel = bass.ds(t * PARTS + (ROWS * grp + part), 1)
            if second:
                return pw[:, c, MERGED[grp].index(quad), channel]
            return nw[:, c, QUAD_TAPS[grp][quad][0], channel]

        def needed_quads(it0, i):
            return it0 + (i // GROUPS - RING // GROUPS + 1 + RING_CREDIT)

        def interior(padded):
            return padded[:, :, 1:1 + H, 1:1 + W]

        def hw(v):
            return v.rearrange("p a (h w) -> p a h w", h=H)

        def diag(j):
            return ring[:, j, 0:HW]

        def weighed(j):
            return ring[:, j, HW:2 * HW]

        def spread(j):
            return misc if j % 2 == 0 else e_ps

        @block.sync
        def _(sp):
            def load(dst, src):
                sp.dma_start(dst, src).then_inc(loaded, 16)

            def column(v):
                return v.rearrange("(p o) -> p o", o=1)

            with nc.allow_non_contiguous_dma(reason="small transposed weights, once"):
                for c, name in enumerate(("L0_conv_w1", "L0_conv_w2")):
                    load(w_raw[c], a[name].rearrange("o i h w -> o (i h w)"))
                for name, src in (("g1", "bn1_gamma"), ("b1", "bn1_beta"), ("m1", "bn1_mean"), ("v1", "bn1_var"),
                                  ("g2", "bn2_gamma"), ("b2", "bn2_beta"), ("m2", "bn2_mean"), ("v2", "bn2_var"),
                                  ("fc2b", "fc2_b")):
                    load(col[name], column(a["L0_conv_" + src]))
                load(col["bh"], column(a["L1_attn_bh"]))
                load(col["wa"], a["L1_attn_Wa"])
                load(col["fc1b"][0:8, :], column(a["L0_conv_fc1_b"]))
                load(wt_sb, a["L1_attn_Wt"])
                load(wx_sb, a["L1_attn_Wx"])
                load(fc1T, a["L0_conv_fc1_w"].rearrange("r c -> c r"))
                load(fc2T[0:8, :], a["L0_conv_fc2_w"].rearrange("c r -> r c"))
                load(row[:, 0, 0:1], a["L1_attn_ba"].rearrange("(o p) -> o p", o=1))
                load(row[:, 1, :], a["L1_ffn_log_weights"].rearrange("(o p) -> o p", o=1))
                load(row[:, 2, :], a["L1_ffn_gumbel"].rearrange("(o p) -> o p", o=1))
                load(mu_raw, a["L1_ffn_M_u"].rearrange("i t d e -> d i t e"))
                load(xn.rearrange("p (n q) -> p n q", n=PAIR), x_dram[0])

            sp.wait_ge(act_setup, ACT_FILT)
            sp.dma_start(filt_dram, phiT).then_inc(filters_stored, 16)

            def next_pair(g):
                sp.wait_ge(x_padded, g)
                sp.dma_start(xn.rearrange("p (n q) -> p n q", n=PAIR),
                             x_dram[bass.ds(g, 1)].rearrange("o p n q -> (o p) n q")).then_inc(x_loaded, 16)

            def store_mid(g, c):
                sp.wait_ge(fin_dve, ((g - 1) * 2 + c + 1) * FIN_DVE)
                sp.dma_start(mid_dram[bass.ds((g - 1) * PAIR + c, 1)].rearrange("o p q -> (o p) q"),
                             tt[:, c, :]).then_inc(mid_stored, 16)

            if pairs > 1:
                next_pair(1)
            with sp.Fori(1, pairs) as g:
                store_mid(g, 0)
                store_mid(g, 1)
                sp.wait_ge(x_padded, g + 1)
                sp.dma_start(xn.rearrange("p (n q) -> p n q", n=PAIR),
                             x_dram[bass.ds((g + 1) % pairs, 1)].rearrange("o p n q -> (o p) n q")).then_inc(x_loaded, 16)
            store_mid(pairs, 0)
            store_mid(pairs, 1)

            sp.wait_ge(filters_stored, 16)
            sp.wait_ge(mid_stored, 16 * n_img)
            sp.wait_ge(fin_dve, n_img * FIN_DVE)
            sp.wait_ge(x_loaded, 16 * pairs)
            for kp in range(NK):
                if kp % 2 == 0:
                    k = kp // 2
                    if k >= 2:
                        sp.wait_ge(m_step, 1 + NLEN + (k - 1) * M_STEPS)
                    for sign, name in enumerate(("plus", "minus")):
                        sp.dma_start(raw[:, k % 2, sign], a["L1_ffn_M_phi_" + name][:, k].rearrange("i d e -> d i e"))\
                            .then_inc(m_loaded[k % 2], 16)
                src = bass.AP(tensor=filt, offset=kp * FROW, ap=[[1, P], [1, FW]])
                sp.dma_start(toep[:, kp, :], src).then_inc(toep_loaded, 16)
            sp.sem_inc(out_stored, 16)
            sp.dma_start(tok, mid_dram[0]).then_inc(tok_loaded, 16)
            with sp.Fori(0, n_img) as b:
                sp.wait_ge(residual_kept, b + 1)
                sp.dma_start(tok, mid_dram[bass.ds((b + 1) % n_img, 1)].rearrange("o p q -> (o p) q")).then_inc(tok_loaded, 16)
                sp.wait_ge(result_ready, b + 1)
                sp.dma_start(out_dram[bass.ds(b, 1)].rearrange("o p q -> (o p) q"), result).then_inc(out_stored, 16)
            sp.wait_ge(out_stored, 16 * (n_img + 1))
            sp.wait_ge(tok_loaded, 16 * (n_img + 1))


        @block.gpsimd
        def _(pool):
            nc.gpsimd.memset(ring[:, 2, :], 0.0).then_inc(consts, 1)
            pool.wait_ge(consts, 1)
            with nc.allow_non_contiguous_dma(reason="filters transposed, once"):
                src = a["L1_ffn_phi"][0:HW, :].rearrange("(t two) k -> two k t", two=2)
                for par in range(2):
                    pool.dma_start(ring[par * NF:(par + 1) * NF, 2, P:P + HALF], src[par]).then_inc(filters_loaded, 16)
                    pool.dma_start(small[par * NF:(par + 1) * NF, 0:1],
                                   a["L1_ffn_sigma"].rearrange("(k o) -> k o", o=1)).then_inc(filters_loaded, 16)
            made = 1
            for buf, val in ((ident, 0.0), (sums, 1.0), (means, 1.0 / P), (nhalf, -0.5), (zeros, 0.0),
                             (ones_hot, 0.0), (wa_hot, 0.0), (ep, OUTSIDE), (xl[:, :, 0:1], 0.0),
                             (xl[:, :, EP - 1:EP], 0.0), (xp, 0.0), (x2p, 0.0)):
                nc.gpsimd.memset(buf, val).then_inc(consts, 1)
                made += 1
            for i in range(4):
                nc.gpsimd.memset(row[:, 7, i:i + 1], float(4 - i)).then_inc(consts, 1)
                made += 1
            pool.wait_ge(consts, made)
            nc.gpsimd.memset(ones_hot[:, ROWS - 1:ROWS], 1.0).then_inc(consts, 1)
            nc.gpsimd.affine_select(out=ident, in_=ident, compare_op=ALU.not_equal, fill=1.0, base=0,
                                    pattern=[[-1, P]], channel_multiplier=1).then_inc(consts, 1)
            made += 2
            assert made == CONSTS

            def boxes(conv_index, src, ready, count):
                s = Steps(box_step, 4, conv_index)
                pool.wait_ge(ready, count)
                pool.wait_ge(sums_closed, conv_index + 1)
                s.link(pool, nc.gpsimd.tensor_tensor(box_rows, src[:, :, :, 0:W], src[:, :, :, 1:1 + W], ALU.add))
                s.link(pool, nc.gpsimd.tensor_tensor(box_rows, box_rows, src[:, :, :, 2:2 + W], ALU.add))
                s.link(pool, nc.gpsimd.tensor_tensor(box, box_rows[:, :, 0:H, :], box_rows[:, :, 1:1 + H, :], ALU.add))
                s.did(nc.gpsimd.tensor_tensor(box, box, box_rows[:, :, 2:2 + H, :], ALU.add))

            with pool.Fori(0, pairs) as g:
                boxes(g * 2, xp, x_padded, g + 1)
                boxes(g * 2 + 1, x2p, x2_ready, g + 1)


        @block.scalar
        def _(act):
            s = Steps(act_setup, 11, 0)
            act.wait_ge(filters_loaded, 64)
            act.wait_ge(consts, CONSTS)
            act.wait_ge(loaded, 16 * NLOADS)
            def seconds(c):
                for grp in range(GROUPS):
                    for which, tap in enumerate(SECOND_TAPS[grp]):
                        o = tap * P + ROWS * grp
                        nc.scalar.activation(pw[:, c, which, ROWS * grp:ROWS * (grp + 1)], acc[:, o:o + ROWS], ACT.Copy)

            s.link(act, nc.scalar.activation(sig, sig, ACT.Sqrt))
            s.link(act, nc.scalar.activation(sig, sig, ACT.Sqrt))
            s.did(nc.scalar.activation(ring[0:NK, 2, P:FROW], ring[0:NK, 2, P:FROW], ACT.Copy, scale=sig))
            act.wait_ge(dve_setup, 2)
            s.did(nc.scalar.activation(col["v1"], col["v1"], ACT.Sqrt))
            s.did(nc.scalar.activation(col["v2"], col["v2"], ACT.Sqrt))
            act.wait_ge(pe_setup, TAPS)
            seconds(0)
            s.did(nc.scalar.activation(nw[:, 0], acc[:, 0:TAPS * P].rearrange("p (t o) -> p t o", t=TAPS), ACT.Copy, scale=-1.0))
            act.wait_ge(pe_setup, 2 * TAPS)
            seconds(1)
            s.did(nc.scalar.activation(nw[:, 1], acc[:, 0:TAPS * P].rearrange("p (t o) -> p t o", t=TAPS), ACT.Copy, scale=-1.0))
            s.did(nc.scalar.activation(wa_hot[:, ROWS - 1:ROWS], col["wa"], ACT.Copy))
            s.did(nc.scalar.activation(col["fc2b"], col["fc2b"], ACT.Copy, scale=0.5))
            act.wait_ge(dve_setup, 5)
            s.did(nc.scalar.activation(row[:, 5, :], row[:, 4, :], ACT.Exp))
            s.did(nc.scalar.activation(interior(xp), xn.rearrange("p (a h w) -> p a h w", a=PAIR, h=H), ACT.Copy))
            assert s.n == 11
            act.wait_ge(act_setup, ACT_SETUP)
            act.wait_ge(dve_setup, DVE_SETUP)
            act.sem_inc(x_padded, 1)
            act.wait_ge(m_step, 1 + NLEN)
            act.wait_ge(filters_stored, 16)

            def loop(g, c, conv, scores):
                mine = ACT_TILES[scores]
                with act.Fori(0, TILES) as t:
                    if conv:
                        it0 = conv_tile(g, c, t) * (PARTS * QUADS)
                        act.wait_ge(relus_used, it0 + RING_CREDIT)
                        nc.scalar.activation(ones_now, ones_hot[:, bass.ds((ROWS - PARTS) - t * PARTS, ROWS + PARTS - 1)],
                                             ACT.Copy).then_inc(hot_ready, 1)
                    for part in range(PARTS):
                        order = []
                        if not scores:
                            order = [("relu", i) for i in mine]
                        else:
                            for qd in range(TQUADS):
                                if conv:
                                    order += [("relu", i) for i in mine if i // GROUPS == qd]
                                order.append(("tanh", qd))
                        for kind, i in order:
                            if kind == "relu":
                                act.wait_ge(relus_used, needed_quads(it0 + part * QUADS, i))
                                nc.scalar.activation(tile(part, i), taps_of(c, QUAD_TAPS[i % GROUPS][i // GROUPS][0]), ACT.Relu,
                                                     bias=weight(c, i, part, t)).then_inc(relu_act, 1)
                            else:
                                r = part * TQUADS + i
                                act.wait_ge(tanhs_used, score_tile(g, c, t) * TILE_TQUADS + (r + 1))
                                for j in range(GROUPS):
                                    nc.scalar.activation(tring[:, (r % 2) * GROUPS + j, :], kT[:, c, :], ACT.Tanh,
                                                         bias=qT[:, c, bass.ds(t * P + (ROWS * j + r), 1)])\
                                        .then_inc(tanh_ready, 1)

            def finish(g, c):
                before = (g - 1) * 2 + c
                act.wait_ge(score_step, (before + 1) * (TILES * SCORE) + 1)
                nc.scalar.activation(expd, scores3, ACT.Exp).then_inc(fin_act, 1)

            def mid(g):
                act.wait_ge(sums_closed, g * 2 + 2)
                for n in range(PAIR):
                    nc.scalar.activation(interior(x2p)[:, n], acc[:, n * HW:(n + 1) * HW].rearrange("p (h w) -> p h w", h=H),
                                         ACT.Relu, bias=col["bi1"], scale=col["sc1"]).then_inc(post_act, 1)
                act.wait_ge(post_act, g * POST_ACT + 2)
                act.sem_inc(x2_ready, 1)

            def post(g):
                s = Steps(post_act, POST_ACT, g)
                s.n = 2
                dve, pe = Steps(post_dve, POST_DVE, g), Steps(post_pe, POST_PE, g)
                act.wait_ge(sums_closed, g * 2 + 3)
                for n in range(PAIR):
                    s.did(nc.scalar.activation(ring[:, 0, n * HW:(n + 1) * HW], acc[:, n * HW:(n + 1) * HW], ACT.Identity,
                                               bias=col["bi2"], scale=col["sc2"], accum_out=pooled[:, n:n + 1]))
                act.wait_ge(pe.sem, pe.at(1))
                s.did(nc.scalar.activation(z1, misc[0:8, 0:PAIR], ACT.Relu, bias=col["fc1b"][0:8, :], scale=1.0 / HW))
                act.wait_ge(pe.sem, pe.at(2))
                s.did(nc.scalar.activation(th, misc[:, BANK:BANK + PAIR], ACT.Tanh, bias=col["fc2b"], scale=0.5))
                act.wait_ge(dve.sem, dve.at(5))
                s.did(nc.scalar.activation(ring[:, 2, :], ring[:, 1, :], ACT.Square))
                act.wait_ge(pe.sem, pe.at(4))
                act.wait_ge(dve.sem, dve.at(6))
                s.did(nc.scalar.activation(ring[:, 3, :], ring[:, 3, :], ACT.Sqrt))
                assert s.n == POST_ACT
                act.wait_ge(pe.sem, pe.at(5))
                nc.scalar.activation(qT, acc[:, :].rearrange("p (a q) -> p a q", a=PAIR), ACT.Identity,
                                     bias=col["bh"]).then_inc(queries_ready, 1)

            def pad_next(g):
                act.wait_ge(post_dve, g * POST_DVE + 4)
                act.wait_ge(x_loaded, (g + 1) * 16)
                nc.scalar.activation(interior(xp), xn.rearrange("p (a h w) -> p a h w", a=PAIR, h=H), ACT.Copy)\
                    .then_inc(x_padded, 1)
                act.wait_ge(post_dve, (g + 1) * POST_DVE)
                act.wait_ge(queries_ready, g + 1)
                act.wait_ge(x_padded, g + 2)

            loop(0, 0, True, False)
            mid(0)
            loop(0, 1, True, False)
            post(0)
            pad_next(0)
            with act.Fori(1, pairs) as g:
                loop(g, 0, True, True)
                mid(g)
                finish(g, 0)
                act.wait_ge(fin_dve, ((g - 1) * 2 + 1) * FIN_DVE)
                loop(g, 1, True, True)
                finish(g, 1)
                act.wait_ge(fin_dve, ((g - 1) * 2 + 2) * FIN_DVE)
                post(g)
                pad_next(g)
            loop(pairs, 0, False, True)
            finish(pairs, 0)
            act.wait_ge(fin_dve, (n_img - 1) * FIN_DVE)
            loop(pairs, 1, False, True)
            finish(pairs, 1)

            def square(b):
                act.wait_ge(ln_dve, b * LN_DVE + 1)
                nc.scalar.activation(ln_b, ln_a, ACT.Square).then_inc(ln_act, 1)

            def root(b):
                act.wait_ge(ln_dve, b * LN_DVE + 2)
                nc.scalar.activation(ln_b, ln_b, ACT.Sqrt).then_inc(ln_act, 1)

            square(0)
            root(0)
            with act.Fori(0, n_img) as b:
                for n in range(NK):
                    act.wait_ge(filt_sums, b * NK + (n + 1))
                    act.wait_ge(filt_mixed, b * NK + (n + 1))
                    nc.scalar.activation(conv_out[:, n % 3, 1, :], acc[:, (n % 2) * HW + HALF:(n % 2) * HW + HW],
                                         ACT.Copy).then_inc(filt_copied_act, 1)
                    if n == AT_SQUARE:
                        square(b + 1)
                    elif n == AT_ROOT:
                        root(b + 1)

        @block.vector
        def _(dve):
            v = nc.vector
            s = Steps(dve_setup, DVE_SETUP, 0)
            dve.wait_ge(loaded, 16 * NLOADS)
            dve.wait_ge(consts, CONSTS)
            s.did(v.tensor_scalar_add(col["v1"], col["v1"], BN_EPS))
            s.did(v.tensor_scalar_add(col["v2"], col["v2"], BN_EPS))
            s.link(dve, v.tensor_tensor(row[:, 3, :], row[:, 1, :], row[:, 2, :], ALU.add))
            s.link(dve, v.tensor_reduce(row[:, 0, 1:2], row[:, 3, :], AX.X, ALU.max))
            s.did(v.tensor_scalar(row[:, 4, :], row[:, 3, :], row[:, 0, 1:2], None, ALU.subtract))
            dve.wait_ge(act_setup, 10)
            s.link(dve, v.tensor_reduce(row[:, 0, 2:3], row[:, 5, :], AX.X, ALU.add))
            s.link(dve, v.reciprocal(row[:, 0, 2:3], row[:, 0, 2:3]))
            s.link(dve, v.tensor_scalar(row[:, 5, :], row[:, 5, :], row[:, 0, 2:3], None, ALU.mult))
            s.link(dve, v.tensor_reduce(row[:, 0, 3:4], row[:, 5, :], AX.X, ALU.max))
            s.link(dve, v.scalar_tensor_tensor(row[:, 6, :], row[:, 5, :], row[:, 0, 3:4], row[:, 7, :], ALU.is_equal, ALU.mult))
            s.link(dve, v.tensor_reduce(row[:, 0, 3:4], row[:, 6, :], AX.X, ALU.max))
            s.link(dve, v.tensor_scalar(row[:, 6, :], row[:, 6, :], row[:, 0, 3:4], None, ALU.is_equal))
            s.link(dve, v.tensor_tensor(row[:, 6, :], row[:, 6, :], row[:, 5, :], ALU.subtract))
            s.did(v.tensor_tensor(row[:, 6, :], row[:, 6, :], row[:, 5, :], ALU.add))
            for c in (0, 1):
                g_, b_, m_, v_ = (col[n + "12"[c]] for n in ("g", "b", "m", "v"))
                sc, bi = col[("sc1", "sc2")[c]], col[("bi1", "bi2")[c]]
                s.did(v.reciprocal(v_, v_))
                for grp in range(GROUPS):
                    rows_ = slice(ROWS * grp, ROWS * (grp + 1))
                    (second,) = SECOND_TAPS[grp]
                    v.tensor_reduce(col["tmp"][rows_, :], w_raw[c][rows_, :].rearrange("p (i t) -> p i t", t=TAPS)[:, :, second],
                                    AX.X, ALU.add)
                s.link(dve, v.tensor_reduce(col["sw"], w_raw[c], AX.X, ALU.add))
                s.link(dve, v.scalar_tensor_tensor(col["sw"], col["tmp"], -2.0, col["sw"], ALU.mult, ALU.add))
                s.link(dve, v.tensor_tensor(v_, v_, g_, ALU.mult))
                v.tensor_scalar(sc, v_, -2.0, None, ALU.mult)
                s.link(dve, v.tensor_tensor(m_, m_, col["sw"], ALU.add))
                s.link(dve, v.tensor_tensor(m_, m_, v_, ALU.mult))
                s.link(dve, v.tensor_tensor(bi, b_, m_, ALU.subtract))
            assert s.n == DVE_SETUP, s.n
            dve.wait_ge(pe_setup, PE_BC)
            v.tensor_copy(col["ba"], misc[:, 0:1])
            v.tensor_copy(wlen, misc[:, BANK:BANK + NLEN]).then_inc(m_step, 1)
            dve.wait_ge(m_step, 1)
            for r in range(NLEN):
                if r == 0:
                    i = v.tensor_scalar(mu[:, :, 0, :], mu_raw[:, 0], wlen[:, 0:1], None, ALU.mult)
                else:
                    i = v.scalar_tensor_tensor(mu[:, :, r, :], mu_raw[:, r], wlen[:, r:r + 1], mu[:, :, r - 1, :], ALU.mult, ALU.add)
                i.then_inc(m_step, 1)
                dve.wait_ge(m_step, 2 + r)
            dve.wait_ge(filters_stored, 16)
            dve.wait_ge(act_setup, 11)

            def score(g, c, t):
                s = Steps(score_step, SCORE, score_tile(g, c, t), 1)
                dve.wait_ge(tanhs_used, (score_tile(g, c, t) + 1) * TILE_TQUADS + 2)
                s.link(dve, v.tensor_scalar(ep[:, 1:1 + HW], e_ps[:, :], col["ba"], None, ALU.add, ALU.max, accum_out=m_cur))
                for j in range(3):
                    last = v.tensor_tensor(prod[:, j, :], ep[:, bass.ds(t * P + j, P)], ident, ALU.mult)
                s.link(dve, last)
                s.link(dve, v.tensor_reduce(e_cur, prod, AX.X, ALU.add))
                s.link(dve, v.tensor_scalar(scores3[:, bass.ds(t, 1), :].rearrange("p o j -> p (o j)"), e_cur, m_cur, None, ALU.subtract))

            def relus(g, c, t, scores, late=None):
                it0 = conv_tile(g, c, t) * (PARTS * QUADS)
                made = dve_relus(g, c, t)
                n = 0
                for part in range(PARTS):
                    for q, work in enumerate(dve_order(scores)):
                        if late is not None and part == 0 and q == RING // GROUPS:
                            late()
                        dve.wait_ge(relus_used, needed_quads(it0 + part * QUADS, GROUPS * q))
                        number = {}
                        for i, which in work:
                            src = taps_of(c, QUAD_TAPS[i % GROUPS][q][which])
                            n += 1
                            if which == 0:
                                v.tensor_scalar(tile(part, i), src, weight(c, i, part, t), 0.0,
                                                ALU.add, ALU.max).then_inc(relu_dve, 1)
                                number[i] = n
                            else:
                                dve.wait_ge(relu_dve, made + number[i])
                                for img in range(PAIR):
                                    last = v.scalar_tensor_tensor(tile(part, i)[:, img], src[:, img], weight(c, i, part, t, True),
                                                                  tile(part, i)[:, img], ALU.max, ALU.add)
                                last.then_inc(relu_dve, 1)

            def loop(g, c, conv, scores):
                if not scores:
                    with dve.Fori(0, TILES) as t:
                        relus(g, c, t, scores)
                elif conv:
                    relus(g, c, 0, scores)
                    with dve.Fori(1, TILES) as t:
                        relus(g, c, t, scores, late=lambda: score(g, c, t - 1))
                    score(g, c, TILES - 1)
                else:
                    with dve.Fori(0, TILES) as t:
                        score(g, c, t)

            def finish(g, c):
                before = (g - 1) * 2 + c
                s = Steps(fin_dve, FIN_DVE, before)
                dve.wait_ge(fin_act, before + 1)
                s.link(dve, v.tensor_reduce(s8, expd, AX.X, ALU.add))
                s.link(dve, v.tensor_scalar_add(s8, s8, ATTN_EPS))
                s.link(dve, v.reciprocal(r8, s8))
                s.link(dve, v.tensor_tensor(probs, expd, r8.rearrange("p (t o) -> p t o", o=1).broadcast_to([P, TILES, 3]), ALU.mult))
                for j in range(3):
                    s.did(v.tensor_tensor(diag(j).rearrange("p (t q) -> p t q", t=TILES),
                                          ident.rearrange("p (o q) -> p o q", o=1).broadcast_to([P, TILES, P]),
                                          probs[:, :, j:j + 1].broadcast_to([P, TILES, P]), ALU.mult))
                for j in range(3):
                    dve.wait_ge(fin_pe, before * FIN_PE + j + 1)
                    s.link(dve, v.tensor_tensor(weighed(j), spread(j)[:, :], xl[:, c, j:j + HW], ALU.mult))
                for j in range(3):
                    s.link(dve, v.tensor_tensor(tt[:, c, :], tt[:, c, :], weighed(j), ALU.add))
                assert s.n == FIN_DVE, s.n

            def post(g):
                s = Steps(post_dve, POST_DVE, g)
                actor, pe = Steps(post_act, POST_ACT, g), Steps(post_pe, POST_PE, g)
                dve.wait_ge(actor.sem, actor.at(6))
                s.link(dve, v.tensor_scalar(gate, th, 0.5, 0.5, ALU.mult, ALU.add))
                if not (isinstance(g, int) and g == 0):
                    dve.wait_ge(mid_stored, g * (16 * PAIR))
                for n in range(PAIR):
                    s.did(v.scalar_tensor_tensor(hw(tt)[:, n], ring[:, 0, n * HW:(n + 1) * HW].rearrange("p (h w) -> p h w", h=H),
                                                 gate[:, n:n + 1], interior(xp)[:, n], ALU.mult, ALU.add))
                dve.wait_ge(post_dve, s.at(3))
                s.did(v.tensor_scalar(tt, tt, 0.0, None, ALU.max))
                dve.wait_ge(pe.sem, pe.at(3))
                s.did(v.tensor_tensor(ring[:, 1, :], tt.rearrange("p a q -> p (a q)"), acc[:, :], ALU.subtract))
                dve.wait_ge(pe.sem, pe.at(4))
                s.did(v.tensor_scalar_add(ring[:, 3, :], acc[:, :], LN_EPS))
                dve.wait_ge(actor.sem, actor.at(8))
                s.link(dve, v.reciprocal(ring[:, 4, :], ring[:, 3, :]))
                s.did(v.tensor_tensor(xl[:, :, 1:1 + HW], ring[:, 1, :].rearrange("p (a q) -> p a q", a=PAIR),
                                      ring[:, 4, :].rearrange("p (a q) -> p a q", a=PAIR), ALU.mult))
                dve.wait_ge(pe.sem, pe.at(6))
                v.tensor_copy(kT[:, 0, :], misc[:, :])
                s.did(v.tensor_copy(kT[:, 1, :], e_ps[:, :]))
                assert s.n == POST_DVE

            dve.sem_inc(score_step, 1)
            for c in (0, 1):
                if c == 0:
                    dve.wait_ge(x_padded, 1)
                else:
                    dve.wait_ge(x2_ready, 1)
                loop(0, c, True, False)
            post(0)
            dve.wait_ge(x_padded, 2)
            with dve.Fori(1, pairs) as g:
                loop(g, 0, True, True)
                finish(g, 0)
                dve.wait_ge(x2_ready, g + 1)
                loop(g, 1, True, True)
                finish(g, 1)
                post(g)
                dve.wait_ge(x_padded, g + 2)
            loop(pairs, 0, False, True)
            finish(pairs, 0)
            loop(pairs, 1, False, True)
            finish(pairs, 1)

            for k in range(NF):
                s = Steps(m_step, M_STEPS, k, 1 + NLEN)
                dve.wait_ge(m_loaded[k % 2], 32 * (k // 2 + 1))
                s.did(v.tensor_tensor(xm[:, 0], raw[:, k % 2, 0], raw[:, k % 2, 1], ALU.add))
                s.link(dve, v.tensor_tensor(xm[:, 1], raw[:, k % 2, 0], raw[:, k % 2, 1], ALU.subtract))
                s.link(dve, v.tensor_scalar(mf[:, k, :, 0, :], xm[:, :, 0, :], wlen[:, 0:1], None, ALU.mult))
                for r in range(1, NLEN):
                    s.link(dve, v.scalar_tensor_tensor(mf[:, k, :, r, :], xm[:, :, r, :], wlen[:, r:r + 1], mf[:, k, :, r - 1, :], ALU.mult, ALU.add))
            v.memset(uT[:, :, 0:1], 0.0)

            def centre(b):
                dve.wait_ge(ln_pe, b * LN_PE + 1)
                v.tensor_tensor(ln_a, tok, e_ps[:, :], ALU.subtract).then_inc(ln_dve, 1)

            def add_eps(b):
                dve.wait_ge(ln_pe, b * LN_PE + 2)
                v.tensor_scalar_add(ln_b, e_ps[:, :], LN_EPS).then_inc(ln_dve, 1)

            def scale(b):
                s = Steps(ln_dve, LN_DVE, b)
                s.n = 2
                dve.wait_ge(ln_act, b * LN_ACT + 2)
                s.link(dve, v.reciprocal(ln_b, ln_b))
                s.link(dve, v.tensor_tensor(uT[:, :, 1:FW].rearrange("p a t -> p t a"),
                                            ln_a.rearrange("p (t a) -> p t a", a=2), ln_b.rearrange("p (t a) -> p t a", a=2), ALU.mult))
                s.did(v.tensor_copy(uR, uT[:, :, HALF:0:-1]))

            def blocks(b):
                dve.wait_ge(ln_pe, b * LN_PE + 3)
                v.tensor_copy(u.rearrange("p a i d -> p (a i d)"), e_ps[:, :]).then_inc(ln_dve, 1)

            for stage in (centre, add_eps, scale, blocks):
                stage(0)
            with dve.Fori(0, n_img) as b:
                dve.wait_ge(tok_loaded, (b + 1) * 16)
                v.tensor_copy(residual, tok).then_inc(residual_kept, 1)
                for n in range(NK):
                    dve.wait_ge(filt_sums, b * NK + (n + 1))
                    dve.wait_ge(filt_mixed, b * NK + (n + 1))
                    v.tensor_copy(conv_out[:, n % 3, 0, :], acc[:, (n % 2) * HW:(n % 2) * HW + HALF]).then_inc(filt_copied_dve, 1)
                    if n == AT_CENTRE:
                        centre(b + 1)
                    elif n == AT_EPS:
                        add_eps(b + 1)
                    elif n == AT_SCALE:
                        scale(b + 1)
                blocks(b + 1)
                dve.wait_ge(residual_kept, b + 1)
                dve.wait_ge(filt_mixed, b * NK + (NK + MIX_CREDIT))
                dve.wait_ge(out_stored, (b + 1) * 16)
                v.tensor_tensor(result.rearrange("p (t a) -> p t a", a=2), residual.rearrange("p (t a) -> p t a", a=2),
                                misc[:, :].rearrange("p (a t) -> p t a", a=2), ALU.add).then_inc(result_ready, 1)
                dve.wait_ge(result_ready, b + 1)

        @block.tensor
        def _(pe):
            mm = nc.tensor.matmul
            zb = zeros[:, :].bitcast(BF16)

            def open_sums(ps, banks):
                for k in range(banks):
                    mm(ps[:, k * BANK:(k + 1) * BANK], zb[:, 0:P], zb[:, 0:BANK], start=True, stop=False, skip_group_check=True)

            pe.wait_ge(loaded, 16 * NLOADS)
            pe.wait_ge(consts, CONSTS)
            for c in (0, 1):
                if c:
                    pe.wait_ge(act_setup, 6)
                w_by_tap = w_raw[c].rearrange("p (i t) -> p t i", t=TAPS)
                for tap in range(TAPS):
                    nc.tensor.transpose(acc[:, tap * P:(tap + 1) * P], w_by_tap[:, tap, :], ident).then_inc(pe_setup, 1)
            mm(misc[:, 0:1], sums[0:1, :], row[:, 0, 0:1], start=True, stop=True).then_inc(pe_setup, 1)
            pe.wait_ge(dve_setup, 14)
            mm(misc[:, BANK:BANK + NLEN], sums[0:1, :], row[:, 6, :], start=True, stop=True).then_inc(pe_setup, 1)
            pe.wait_ge(act_setup, 11)
            pe.sem_inc(relus_used, RING_CREDIT)
            pe.sem_inc(tanhs_used, 2)
            pe.sem_inc(sums_closed, 1)
            pe.sem_inc(filt_mixed, MIX_CREDIT)
            pe.wait_ge(dve_setup, DVE_SETUP)

            def loop(g, c, conv, scores):
                mine = ACT_TILES[scores]
                if conv:
                    open_sums(acc, PAIRPOS // BANK)
                with pe.Fori(0, TILES) as t:
                    if conv:
                        it0 = conv_tile(g, c, t) * PARTS
                        pe.wait_ge(hot_ready, conv_tile(g, c, t) + 1)
                    for part in range(PARTS):
                        assert QUADS == TQUADS
                        order = [(kind, q) for q in range(QUADS) for kind, there in (("relu", conv), ("tanh", scores)) if there]
                        for kind, q in order:
                            if kind == "relu":
                                n_act = sum(i < GROUPS * (q + 1) for i in mine)
                                n_dve = sum(len(work) for work in dve_order(scores)[:q + 1])
                                if any(i // GROUPS == q for i in mine):
                                    pe.wait_ge(relu_act, act_relus(g, c, t) + (part * ACT_SHARE[scores] + n_act))
                                pe.wait_ge(relu_dve, dve_relus(g, c, t) + (part * DVE_SHARE[scores] + n_dve))
                                hot = ones_now[:, PARTS - 1 - part:PARTS - 1 - part + ROWS]
                                for k in range(PAIRPOS // BANK):
                                    for grp in range(GROUPS):
                                        last = mm(acc[ROWS * grp:ROWS * (grp + 1), k * BANK:(k + 1) * BANK], hot,
                                                  buffer(part, GROUPS * q + grp)[:, k * BANK:(k + 1) * BANK],
                                                  start=False, stop=False, skip_group_check=True)
                                last.then_inc(relus_used, 1)
                            else:
                                r = part * TQUADS + q
                                if r == 0:
                                    pe.wait_ge(score_step, score_tile(g, c, t) * SCORE + 1)
                                    open_sums(e_ps, HW // BANK)
                                pe.wait_ge(tanh_ready, score_tile(g, c, t) * (TILE_TQUADS * GROUPS) + GROUPS * (r + 1))
                                hot = wa_hot[:, ROWS - 1 - r:2 * ROWS - 1 - r]
                                for k in range(HW // BANK):
                                    for j in range(GROUPS):
                                        last = mm(e_ps[ROWS * j:ROWS * (j + 1), k * BANK:(k + 1) * BANK], hot,
                                                  tring[:, (r % 2) * GROUPS + j, k * BANK:(k + 1) * BANK],
                                                  start=False, stop=False, skip_group_check=True)
                                last.then_inc(tanhs_used, 1)

            def close_sums(g, c):
                pe.wait_ge(box_step, ((g * 2 + c) + 1) * 4)
                for k in range(PAIRPOS // BANK):
                    rows = BANK // W
                    last = mm(acc[:, k * BANK:(k + 1) * BANK], nhalf,
                              box[:, k * rows // H, (k * rows) % H:(k * rows) % H + rows, :],
                              start=False, stop=True, skip_group_check=True)
                last.then_inc(sums_closed, 1)

            def finish(g, c):
                before = (g - 1) * 2 + c
                for j in range(3):
                    pe.wait_ge(fin_dve, before * FIN_DVE + (5 + j if j < 2 else 8))
                    for k in range(HW // BANK):
                        last = mm(spread(j)[:, k * BANK:(k + 1) * BANK], sums, diag(j)[:, k * BANK:(k + 1) * BANK],
                                  start=True, stop=True)
                    last.then_inc(fin_pe, 1)
                pe.wait_ge(fin_dve, (before + 1) * FIN_DVE)

            def post(g):
                s = Steps(post_pe, POST_PE, g)
                actor, dve = Steps(post_act, POST_ACT, g), Steps(post_dve, POST_DVE, g)
                pe.wait_ge(actor.sem, actor.at(4))
                s.did(mm(misc[0:8, 0:PAIR], fc1T, pooled, start=True, stop=True))
                pe.wait_ge(actor.sem, actor.at(5))
                s.did(mm(misc[:, BANK:BANK + PAIR], fc2T[0:8, :], z1, start=True, stop=True))
                t2 = tt.rearrange("p a q -> p (a q)")

                def wide(stationary, moving, targets):
                    for k, o in enumerate(targets):
                        last = mm(o, stationary, moving[k], start=True, stop=True)
                    return last

                acc_banks = [acc[:, k * BANK:(k + 1) * BANK] for k in range(PAIRPOS // BANK)]
                pe.wait_ge(dve.sem, dve.at(4))
                s.did(wide(means, [t2[:, k * BANK:(k + 1) * BANK] for k in range(4)], acc_banks))
                pe.wait_ge(actor.sem, actor.at(7))
                s.did(wide(means, [ring[:, 2, k * BANK:(k + 1) * BANK] for k in range(4)], acc_banks))
                pe.wait_ge(dve.sem, dve.at(8))
                tokens = [xl[:, n, 1 + k * BANK:1 + (k + 1) * BANK] for n in range(PAIR) for k in range(HW // BANK)]
                s.did(wide(wt_sb, tokens, acc_banks))
                s.did(wide(wx_sb, tokens, [p[:, k * BANK:(k + 1) * BANK] for p in (misc, e_ps) for k in range(HW // BANK)]))
                pe.wait_ge(queries_ready, g + 1)
                pe.wait_ge(dve.sem, dve.at(9))

            loop(0, 0, True, False)
            close_sums(0, 0)
            pe.wait_ge(x2_ready, 1)
            loop(0, 1, True, False)
            close_sums(0, 1)
            post(0)
            with pe.Fori(1, pairs) as g:
                loop(g, 0, True, True)
                close_sums(g, 0)
                finish(g, 0)
                pe.wait_ge(x2_ready, g + 1)
                loop(g, 1, True, True)
                close_sums(g, 1)
                finish(g, 1)
                post(g)
            loop(pairs, 0, False, True)
            finish(pairs, 0)
            loop(pairs, 1, False, True)
            finish(pairs, 1)

            pe.wait_ge(toep_loaded, 16 * NK)
            pe.wait_ge(m_step, 1 + NLEN + NF * M_STEPS)

            def average(b, src):
                for k in range(HW // BANK):
                    last = mm(e_ps[:, k * BANK:(k + 1) * BANK], means, src[:, k * BANK:(k + 1) * BANK], start=True, stop=True)
                last.then_inc(ln_pe, 1)

            def mean(b):
                pe.wait_ge(tok_loaded, (b + 1) * 16)
                if not isinstance(b, int):
                    pe.wait_ge(ln_dve, b * LN_DVE)
                average(b, tok)

            def variance(b):
                pe.wait_ge(ln_act, b * LN_ACT + 1)
                average(b, ln_b)

            def transposes(b):
                pe.wait_ge(ln_dve, b * LN_DVE + 5)
                for par in range(2):
                    for i in range(TB):
                        last = nc.tensor.transpose(e_ps[:, (par * TB + i) * P:(par * TB + i + 1) * P],
                                                   uR[:, par, (TB - 1 - i) * P:(TB - i) * P], ident)
                last.then_inc(ln_pe, 1)

            for stage in (mean, variance, transposes):
                stage(0)
            with pe.Fori(0, n_img) as b:
                def recent():
                    for par in range(2):
                        for tap in range(3):
                            src, back = (par - tap) % 2, (tap + 1 - par) // 2
                            for r, (lo, hi) in enumerate(SEGS):
                                mm(misc[:, par * HALF + lo:par * HALF + hi], mu[:, tap, r, :], uT[:, src, 1 + lo - back:1 + hi - back],
                                   start=(tap == 0 and r == 0), stop=False, skip_group_check=True)

                pe.wait_ge(ln_dve, (b + 1) * LN_DVE)

                def filter_sums(n):
                    k, odd = divmod(n, 2)
                    f = toep[:, odd * NF + k, :]
                    o0 = (n % 2) * HW
                    if n >= 2:
                        pe.wait_ge(filt_copied_dve, b * NK + (n - 1))
                        pe.wait_ge(filt_copied_act, b * NK + (n - 1))
                    for par in range(2):
                        src = par ^ odd
                        lead = 0 if (odd and par == 0) else 1
                        for i in range(TB):
                            last = mm(acc[:, o0 + par * HALF + i * P:o0 + (par + 1) * HALF], u[:, src, i, :],
                                      f[:, lead:lead + HALF - i * P], start=(i == 0), stop=(i == TB - 1), skip_group_check=True)
                    last.then_inc(filt_sums, 1)

                def mix(n):
                    k, odd = divmod(n, 2)
                    pe.wait_ge(filt_copied_dve, b * NK + (n + 1))
                    pe.wait_ge(filt_copied_act, b * NK + (n + 1))
                    for par in range(2):
                        for r, (lo, hi) in enumerate(SEGS):
                            last = mm(misc[:, par * HALF + lo:par * HALF + hi], mf[:, k, odd, r, :], conv_out[:, n % 3, par, lo:hi],
                                      start=False, stop=(n == NK - 1), skip_group_check=True)
                    last.then_inc(filt_mixed, 1)

                for n in range(NK):
                    filter_sums(n)
                    if n == 0:
                        pe.wait_ge(residual_kept, b + 1)
                        recent()
                    else:
                        mix(n - 1)
                    if n == AT_MEAN:
                        mean(b + 1)
                    elif n == AT_VAR:
                        variance(b + 1)
                    elif n == AT_TRANSPOSE:
                        transposes(b + 1)
                mix(NK - 1)


_NAMES = ["x", "L0_conv_w1", "L0_conv_bn1_gamma", "L0_conv_bn1_beta", "L0_conv_bn1_mean", "L0_conv_bn1_var",
          "L0_conv_w2", "L0_conv_bn2_gamma", "L0_conv_bn2_beta", "L0_conv_bn2_mean", "L0_conv_bn2_var",
          "L0_conv_fc1_w", "L0_conv_fc1_b", "L0_conv_fc2_w", "L0_conv_fc2_b", "L1_attn_Wt", "L1_attn_Wx",
          "L1_attn_Wa", "L1_attn_bh", "L1_attn_ba", "L1_ffn_sigma", "L1_ffn_phi", "L1_ffn_M_u",
          "L1_ffn_M_phi_plus", "L1_ffn_M_phi_minus", "L1_ffn_log_weights", "L1_ffn_gumbel"]


def kernel(**inputs):
    import numpy as np
    import concourse.bacc as bacc
    from concourse.bass_utils import run_bass_kernel_spmd

    nc = bacc.Bacc("TRN2", target_bir_lowering=False, num_devices=1)
    arrays, aps = {}, {}
    for name in _NAMES:
        arr = np.ascontiguousarray(inputs[name])
        arrays["in_" + name] = arr
        aps[name] = nc.dram_tensor("in_" + name, arr.shape, mybir.dt.from_np(arr.dtype), kind="ExternalInput").ap()
    out = nc.dram_tensor("out", arrays["in_x"].shape, FP32, kind="ExternalOutput").ap()
    build(nc, aps, out)
    r = run_bass_kernel_spmd(nc, [arrays], core_ids=[0])
    return r.results[0]["out"]
```
